# Optimizing a Trainium2 kernel written in Bass

```python
import numpy as np
import jax
import jax.numpy as jnp

def _softmax(x, axis=-1):
    return jax.nn.softmax(x, axis=axis)

def _gelu(x):
    return jax.nn.gelu(x, approximate=True)

def _silu(x):
    return jax.nn.silu(x)

def _sigmoid(x):
    return jax.nn.sigmoid(x)

def _layernorm(x, axis=-1, eps=1e-05):
    m = jnp.mean(x, axis=axis, keepdims=True)
    v = jnp.var(x, axis=axis, keepdims=True)
    return (x - m) / jnp.sqrt(v + eps)

def _scatter_add(tgt, idx, src, axis=0):
    return tgt.at[idx].add(src)

def _segment_sum(src, seg, n):
    return jax.ops.segment_sum(src, seg, n)
kernel_name = 'mk_vit_tower_d1_tok_img256_r4_677264'

def setup_inputs(seed: int=0):
    np.random.seed(seed)
    _w = jnp.asarray

    def _rec_inputs():
        import jax
        import jax.numpy as jnp
        _rk = jax.random.key(seed)
        x = 7.22013e-05 + 1.00017 * jax.random.normal(jax.random.fold_in(_rk, 1), (8, 64, 64, 64), jnp.float32)
        return x
    x = _rec_inputs()

    def _L0_tok_setup():
        import jax, jax.numpy as jnp
        import numpy as np
        K = 3
        PAD = (K - 1) // 2
        BN_EPS = 1e-05

        def _unfold(x):
            b, c, h, w = x.shape
            xp = jnp.pad(x, ((0, 0), (0, 0), (PAD, PAD), (PAD, PAD)))
            shifts = [xp[:, :, i:i + h, j:j + w] for i in range(K) for j in range(K)]
            return jnp.stack(shifts, axis=2)
        key = jax.random.key(seed)
        ks = jax.random.split(key, 4)
        b, c, h, w = (8, 64, 64, 64)
        cr = c // 4
        x = jax.random.normal(ks[0], (b, c, h, w), dtype=jnp.float32)
        conv1_w = jax.random.normal(ks[1], (cr, c), dtype=jnp.float32) * (1.0 / np.sqrt(c))
        conv1_b = jnp.zeros((cr,), dtype=jnp.float32)
        bn_gamma = jnp.ones((cr,), dtype=jnp.float32)
        bn_beta = jnp.zeros((cr,), dtype=jnp.float32)
        bn_mean = jnp.zeros((cr,), dtype=jnp.float32)
        bn_var = jnp.ones((cr,), dtype=jnp.float32)
        conv2_w = jax.random.normal(ks[2], (K * K, cr), dtype=jnp.float32) * (1.0 / np.sqrt(cr))
        conv2_b = jnp.zeros((K * K,), dtype=jnp.float32)
        return {'x': x, 'conv1_w': conv1_w, 'conv1_b': conv1_b, 'bn_gamma': bn_gamma, 'bn_beta': bn_beta, 'bn_mean': bn_mean, 'bn_var': bn_var, 'conv2_w': conv2_w, 'conv2_b': conv2_b}
    _L0_tok_all = _L0_tok_setup()
    _L0_tok_in = {k: v for k, v in _L0_tok_all.items() if k in ('conv1_w', 'conv1_b', 'bn_gamma', 'bn_beta', 'bn_mean', 'bn_var', 'conv2_w', 'conv2_b')}
    del _L0_tok_all

    def _L0_attn_setup():
        import jax, jax.numpy as jnp
        import numpy as np
        NUM_HEADS = 8
        LOCAL_WINDOW = 16
        NEG_INF = -10000000000.0
        key = jax.random.key(seed)
        k0, k1, k2 = jax.random.split(key, 3)
        B, N, C = (2, 1024, 64)
        x = jax.random.normal(k0, (B, N, C), dtype=jnp.float32)
        w_qkv = jax.random.normal(k1, (C, 3 * C), dtype=jnp.float32) * 0.02
        w_proj = jax.random.normal(k2, (C, C), dtype=jnp.float32) * 0.02
        b_proj = jnp.zeros((C,), dtype=jnp.float32)
        return {'x': x, 'w_qkv': w_qkv, 'w_proj': w_proj, 'b_proj': b_proj}
    _L0_attn_all = _L0_attn_setup()
    _L0_attn_in = {k: v for k, v in _L0_attn_all.items() if k in ('w_qkv', 'w_proj', 'b_proj')}
    del _L0_attn_all

    def _L0_ffn_setup():
        import jax, jax.numpy as jnp
        import numpy as np
        E, D, H, TOP_K = (6, 64, 64, 2)
        ROUTER_H = D // 2
        key = jax.random.key(seed)
        ks = jax.random.split(key, 12)
        s = 1.0 / np.sqrt(D)
        sh = 1.0 / np.sqrt(H)
        sr = 1.0 / np.sqrt(ROUTER_H)
        return {'features': jax.random.normal(ks[0], (8, 1024, D), dtype=jnp.float32), 'router_w1': jax.random.uniform(ks[1], (D, ROUTER_H), jnp.float32, -s, s), 'router_b1': jnp.zeros((ROUTER_H,), jnp.float32), 'router_w2': jax.random.uniform(ks[2], (ROUTER_H, E), jnp.float32, -sr, sr), 'router_b2': jnp.zeros((E,), jnp.float32), 'expert_w1': jax.random.uniform(ks[3], (E, D, H), jnp.float32, -s, s), 'expert_b1': jnp.zeros((E, H), jnp.float32), 'expert_w2': jax.random.uniform(ks[4], (E, H, H), jnp.float32, -sh, sh), 'expert_b2': jnp.zeros((E, H), jnp.float32), 'expert_w3': jax.random.uniform(ks[5], (E, H, D), jnp.float32, -sh, sh), 'expert_b3': jnp.zeros((E, D), jnp.float32)}
    _L0_ffn_all = _L0_ffn_setup()
    _L0_ffn_in = {k: v for k, v in _L0_ffn_all.items() if k in ('router_w1', 'router_b1', 'router_w2', 'router_b2', 'expert_w1', 'expert_b1', 'expert_w2', 'expert_b2', 'expert_w3', 'expert_b3')}
    del _L0_ffn_all
    return {'x': x, 'L0_tok_conv1_w': _L0_tok_in['conv1_w'], 'L0_tok_conv1_b': _L0_tok_in['conv1_b'], 'L0_tok_bn_gamma': _L0_tok_in['bn_gamma'], 'L0_tok_bn_beta': _L0_tok_in['bn_beta'], 'L0_tok_bn_mean': _L0_tok_in['bn_mean'], 'L0_tok_bn_var': _L0_tok_in['bn_var'], 'L0_tok_conv2_w': _L0_tok_in['conv2_w'], 'L0_tok_conv2_b': _L0_tok_in['conv2_b'], 'L0_attn_w_qkv': _L0_attn_in['w_qkv'], 'L0_attn_w_proj': _L0_attn_in['w_proj'], 'L0_attn_b_proj': _L0_attn_in['b_proj'], 'L0_ffn_router_w1': _L0_ffn_in['router_w1'], 'L0_ffn_router_b1': _L0_ffn_in['router_b1'], 'L0_ffn_router_w2': _L0_ffn_in['router_w2'], 'L0_ffn_router_b2': _L0_ffn_in['router_b2'], 'L0_ffn_expert_w1': _L0_ffn_in['expert_w1'], 'L0_ffn_expert_b1': _L0_ffn_in['expert_b1'], 'L0_ffn_expert_w2': _L0_ffn_in['expert_w2'], 'L0_ffn_expert_b2': _L0_ffn_in['expert_b2'], 'L0_ffn_expert_w3': _L0_ffn_in['expert_w3'], 'L0_ffn_expert_b3': _L0_ffn_in['expert_b3']}

def reference(x, L0_tok_conv1_w, L0_tok_conv1_b, L0_tok_bn_gamma, L0_tok_bn_beta, L0_tok_bn_mean, L0_tok_bn_var, L0_tok_conv2_w, L0_tok_conv2_b, L0_attn_w_qkv, L0_attn_w_proj, L0_attn_b_proj, L0_ffn_router_w1, L0_ffn_router_b1, L0_ffn_router_w2, L0_ffn_router_b2, L0_ffn_expert_w1, L0_ffn_expert_b1, L0_ffn_expert_w2, L0_ffn_expert_b2, L0_ffn_expert_w3, L0_ffn_expert_b3):
    import jax
    import jax.numpy as jnp

    def _L0_tok_ref(x, conv1_w, conv1_b, bn_gamma, bn_beta, bn_mean, bn_var, conv2_w, conv2_b):
        import jax, jax.numpy as jnp
        import numpy as np
        K = 3
        PAD = (K - 1) // 2
        BN_EPS = 1e-05

        def _unfold(x):
            b, c, h, w = x.shape
            xp = jnp.pad(x, ((0, 0), (0, 0), (PAD, PAD), (PAD, PAD)))
            shifts = [xp[:, :, i:i + h, j:j + w] for i in range(K) for j in range(K)]
            return jnp.stack(shifts, axis=2)
        b, c, h, w = x.shape
        y = jnp.einsum('oc,bchw->bohw', conv1_w, x) + conv1_b[None, :, None, None]
        y = (y - bn_mean[None, :, None, None]) * (bn_gamma[None, :, None, None] * jax.lax.rsqrt(bn_var + BN_EPS)[None, :, None, None]) + bn_beta[None, :, None, None]
        y = jax.nn.relu(y)
        wdyn = jnp.einsum('ok,bkhw->bohw', conv2_w, y) + conv2_b[None, :, None, None]
        patches = _unfold(x)
        out = jnp.einsum('bckhw,bkhw->bchw', patches, wdyn)
        return out.reshape(b, h * w, c)

    def _L0_attn_ref(x, w_qkv, w_proj, b_proj):
        import jax, jax.numpy as jnp
        import numpy as np
        NUM_HEADS = 8
        LOCAL_WINDOW = 16
        NEG_INF = -10000000000.0
        B, N, C = x.shape
        H = NUM_HEADS
        hd = C // H
        scale = hd ** (-0.5)
        qkv = (x @ w_qkv).reshape(B, N, 3, H, hd).transpose(2, 0, 3, 1, 4)
        q, k, v = (qkv[0], qkv[1], qkv[2])
        std = jnp.std(x, axis=-1, ddof=1)
        diff = jnp.mean(jnp.abs(x[:, 1:] - x[:, :-1]), axis=-1)
        grad = jnp.concatenate([jnp.zeros((B, 1), x.dtype), diff], axis=1)
        density = (std + grad) * 0.5
        threshold = jnp.mean(density) + 0.5 * jnp.std(density, ddof=1)
        high_info = density > threshold
        pos = jnp.arange(N)
        local = jnp.abs(pos[None, :] - pos[:, None]) < LOCAL_WINDOW
        mask = jnp.where(local[None, :, :] | high_info[:, None, :], 0.0, NEG_INF)
        attn = jnp.einsum('bhid,bhjd->bhij', q, k) * scale + mask[:, None, :, :]
        attn = jax.nn.softmax(attn, axis=-1)
        out = jnp.einsum('bhij,bhjd->bhid', attn, v)
        out = out.transpose(0, 2, 1, 3).reshape(B, N, C)
        return out @ w_proj + b_proj

    def _L0_ffn_ref(features, router_w1, router_b1, router_w2, router_b2, expert_w1, expert_b1, expert_w2, expert_b2, expert_w3, expert_b3):
        import jax, jax.numpy as jnp
        import numpy as np
        E, D, H, TOP_K = (6, 64, 64, 2)
        ROUTER_H = D // 2
        rh = jax.nn.relu(features @ router_w1 + router_b1)
        expert_logits = jax.nn.softmax(rh @ router_w2 + router_b2, axis=-1)
        top_w, top_i = jax.lax.top_k(expert_logits, TOP_K)
        routing_weights = jax.nn.softmax(top_w, axis=-1)
        h1 = jax.nn.relu(jnp.einsum('bsd,edh->bseh', features, expert_w1) + expert_b1)
        h2 = jax.nn.relu(jnp.einsum('bseh,ehf->bsef', h1, expert_w2) + expert_b2)
        expert_out = jnp.einsum('bsef,efo->bseo', h2, expert_w3) + expert_b3
        sel = jnp.take_along_axis(expert_out, top_i[:, :, :, None], axis=2)
        combined = jnp.sum(sel * routing_weights[..., None], axis=2)
        return combined
    h = _L0_tok_ref(x, L0_tok_conv1_w, L0_tok_conv1_b, L0_tok_bn_gamma, L0_tok_bn_beta, L0_tok_bn_mean, L0_tok_bn_var, L0_tok_conv2_w, L0_tok_conv2_b)
    h = h + _L0_attn_ref(_layernorm(h, axis=-1), L0_attn_w_qkv, L0_attn_w_proj, L0_attn_b_proj)
    h = h + _L0_ffn_ref(_layernorm(h, axis=-1), L0_ffn_router_w1, L0_ffn_router_b1, L0_ffn_router_w2, L0_ffn_router_b2, L0_ffn_expert_w1, L0_ffn_expert_b1, L0_ffn_expert_w2, L0_ffn_expert_b2, L0_ffn_expert_w3, L0_ffn_expert_b3)
    return h

_drawn_inputs = setup_inputs


def setup_inputs(seed=0):
    import zlib

    import numpy as np

    out = dict(_drawn_inputs(seed))
    spreads = {'L0_tok_conv1_b': (0.0, 0.1),
     'L0_tok_bn_gamma': (1.0, 0.2),
     'L0_tok_bn_beta': (0.0, 0.1),
     'L0_tok_bn_mean': (0.0, 0.1),
     'L0_tok_bn_var': (1.0, 0.2),
     'L0_tok_conv2_b': (0.0, 0.1),
     'L0_attn_b_proj': (0.0, 0.1),
     'L0_ffn_router_b1': (0.0, 0.4),
     'L0_ffn_router_b2': (0.0, 0.274),
     'L0_ffn_expert_b1': (0.0, 0.8),
     'L0_ffn_expert_b2': (0.0, 0.584),
     'L0_ffn_expert_b3': (0.0, 0.1)}
    factors = {'L0_attn_w_qkv': 8.0, 'L0_attn_w_proj': 8.0}
    for name, (base, spread) in spreads.items():
        noise = np.random.default_rng([zlib.crc32(name.encode()), seed]).standard_normal(out[name].shape)
        drawn = base * np.exp(spread * noise) if base else spread * noise
        out[name] = jnp.asarray(drawn.astype(out[name].dtype))
    for name, factor in factors.items():
        out[name] = (out[name] * factor).astype(out[name].dtype)
    return out
```

```python
import concourse.bass as bass
from concourse import mybir
from contextlib import ExitStack

FP32 = mybir.dt.float32
BF16 = mybir.dt.bfloat16
I32 = mybir.dt.int32
U32 = mybir.dt.uint32
ALU = mybir.AluOpType
ACT = mybir.ActivationFunctionType
AX = mybir.AxisListType
ds = bass.ds

B, C, H, W = 8, 64, 64, 64
NTOK, D = H * C, W
NH, HD = 8, 8
E, FH, RH = 6, 64, 32
K2 = 9
CR = C // 4
PAIRS = B // 2
EPS = 1e-5
WINDOW = 16
NEG = -1.0e10
ITER = 256
PADT = WINDOW
TP = NTOK + 2 * PADT


PRIME = 32


class Sems:

    def __init__(self, nc, ctx):
        self.nc, self.ctx, self.all = nc, ctx, []
        self.passed = ctx.enter_context(nc.semaphore("passed"))

    def __call__(self, name):
        self.all.append(self.ctx.enter_context(self.nc.semaphore(name)))
        return self.all[-1]

    def prime(self):
        with self.nc.Block() as block:
            @block.sync
            def _(sp):
                for s in self.all:
                    sp.sem_inc(s, PRIME)

    def settle(self, eng):
        eng.sem_inc(self.passed, 1)


class Steps:

    def __init__(self, sems, eng, sem, base):
        self.sems, self.eng, self.sem, self.base, self.n = sems, eng, sem, base, 0

    def __call__(self, instruction):
        self.n += 1
        instruction.then_inc(self.sem, 1)
        self.eng.wait_ge(self.sem, PRIME + self.base + self.n)
        if not isinstance(self.base, int):
            self.sems.settle(self.eng)


def conv_norm(nc, d, keep):
    xn_all, std2, grad = keep["xn_all"], keep["std2"], keep["grad"]
    CD = 46
    HALF = 32 * K2
    x_h = d["x"].rearrange("(p b2) c h w -> p b2 h c w", b2=2)
    x_c = d["x"].rearrange("(p b2) c h w -> p (b2 c) (h w)", b2=2)
    h_v = d["h_dram"].rearrange("(p b2) (c h) w -> p b2 h c w", b2=2, h=H)
    xn_v = d["tok_dram"][0:B * NTOK].rearrange("(p b2 c h) w -> p b2 h c w", b2=2, h=H, c=C)
    with ExitStack() as ctx:
        sb = lambda n, s, t=FP32: ctx.enter_context(nc.sbuf_tensor(n, s, t))
        pb = lambda n, s, t=FP32: ctx.enter_context(nc.psum_tensor(n, s, t))
        sem = Sems(nc, ctx)
        settle = sem.settle
        xs = sb("xs", [128, 3, C, W + 2])
        xc = sb("xc", [128, H * W])
        w1 = sb("w1", [128, 64])
        w2 = sb("w2", [64, 2, K2])
        bn = sb("bn", [64, 8])
        y = sb("y", [64, H * W])
        wd = sb("wd", [128, K2, W])
        prod = sb("prod", [128, C, W])
        hb = sb("hb", [128, C, W])
        bp = sb("bp", [128, D])
        rows = sb("rows", [128, 4, C])
        shift = sb("shift", [128, 2, 128])
        c1 = pb("c1", [128, 2, 512])
        c2 = pb("c2", [128, 2, 512])
        df = pb("df", [128, 2, 1024])
        s_w, s_set, s_bn, s_x, s_xc = sem("s_w"), sem("s_set"), sem("s_bn"), sem("s_x"), sem("s_xc")
        s_y1, s_y, s_w2, s_wd = sem("s_y1"), sem("s_y"), sem("s_w2"), sem("s_wd")
        s_dch, s_pch = sem("s_dch"), sem("s_pch")
        s_conv_v, s_conv_p, s_hb, s_mean = sem("s_conv_v"), sem("s_conv_p"), sem("s_hb"), sem("s_mean")
        s_cen_v, s_cen_p, s_sq, s_rstd = sem("s_cen_v"), sem("s_cen_p"), sem("s_sq"), sem("s_rstd")
        s_xn_v, s_xn_p, s_df, s_gr = sem("s_xn_v"), sem("s_xn_p"), sem("s_df"), sem("s_gr")
        s_hst, s_xst, s_var, s_root = sem("s_hst"), sem("s_xst"), sem("s_var"), sem("s_root")
        sem.prime()
        block = ctx.enter_context(nc.Block())
        W_DMAS = 2 + 2 + 2 + 10 + 1

        @block.sync
        def _(sp):
            sp.wait_ge(s_set, PRIME + 3)
            with nc.allow_non_contiguous_dma(reason="small weights, transposed once"):
                for b2 in range(2):
                    sp.dma_start(w1[64 * b2:64 * b2 + C, 32 * b2:32 * b2 + CR],
                                 d["conv1_w"].rearrange("o c -> c o")).then_inc(s_w, 16)
                    sp.dma_start(w2[32 * b2:32 * b2 + CR, b2, :],
                                 d["conv2_w"].rearrange("k o -> o k")).then_inc(s_w, 16)
                    sp.dma_start(w2[32 * b2 + CR:32 * b2 + CR + 1, b2, :],
                                 d["conv2_b"].rearrange("(a k) -> a k", a=1)).then_inc(s_w, 16)
                    for i, n in enumerate(["conv1_b", "bn_gamma", "bn_beta", "bn_mean", "bn_var"]):
                        sp.dma_start(bn[32 * b2:32 * b2 + CR, i:i + 1],
                                     d[n].rearrange("(o a) -> o a", a=1)).then_inc(s_w, 16)
                sp.dma_start(bp[:, :], d["b_proj"].rearrange("(a k) -> a k", a=1).to_broadcast([128, D])
                             ).then_inc(s_w, 16)
            with sp.Fori(0, PAIRS) as p:
                sp.wait_ge(s_y1, PRIME + p * 8)
                settle(sp)
                sp.dma_start(xc[:, :], x_c[ds(p, 1)].rearrange("a q n -> (a q) n")).then_inc(s_xc, 16)
                sp.wait_ge(s_conv_v, PRIME + p)
                sp.wait_ge(s_conv_p, PRIME + p)
                settle(sp)
                for b2 in range(2):
                    for i in range(3):
                        h0, h1 = max(0, 1 - i), min(H, H + 1 - i)
                        src = x_h[ds(p, 1), b2, h0 + i - 1:h1 + i - 1].rearrange("a h c w -> (a h) c w")
                        sp.dma_start(xs[64 * b2 + h0:64 * b2 + h1, i, :, 1:1 + W], src).then_inc(s_x, 16)
            sp.wait_ge(s_x, PRIME + PAIRS * 96)

        @block.scalar
        def _(act):
            act.wait_ge(s_var, PRIME + 1)
            nc.scalar.activation(bn[:, 7:8], bn[:, 7:8], ACT.Sqrt).then_inc(s_root, 1)
            act.wait_ge(s_bn, PRIME + 1)
            with act.Fori(0, PAIRS) as p:
                act.wait_ge(s_w2, PRIME + p * 2)
                settle(act)
                for j in range(8):
                    act.wait_ge(s_y1, PRIME + p * 8 + j + 1)
                    settle(act)
                    nc.scalar.activation(y[:, 512 * j:512 * j + 512], c1[0:64, j % 2, :], ACT.Relu,
                                         bias=bn[:, 6:7], scale=bn[:, 5:6]).then_inc(s_y, 1)
                act.wait_ge(s_conv_v, PRIME + p)
                act.wait_ge(s_conv_p, PRIME + p)
                settle(act)
                for j in range(2):
                    act.wait_ge(s_w2, PRIME + p * 2 + j + 1)
                    settle(act)
                    nc.scalar.copy(wd[:, :, 32 * j:32 * j + 32],
                                   c2[:, j, 0:HALF].rearrange("p (w k) -> p k w", k=K2)).then_inc(s_wd, 1)
                act.wait_ge(s_hb, PRIME + p + 1)
                settle(act)
                for b2 in range(2):
                    act.dma_start(h_v[ds(p, 1), b2].rearrange("a h c w -> (a h) c w"),
                                  hb[64 * b2:64 * b2 + 64]).then_inc(s_hst, 16)
                act.wait_ge(s_cen_v, PRIME + p + 1)
                act.wait_ge(s_cen_p, PRIME + p + 1)
                settle(act)
                nc.scalar.activation(prod[:, :, :], xn_all[:, ds(p, 1), C:].rearrange("p a n -> p (a n)"),
                                     ACT.Square).then_inc(s_sq, 1)
                act.wait_ge(s_var, PRIME + p + 2)
                settle(act)
                nc.scalar.activation(rows[:, 3, :], rows[:, 3, :], ACT.Sqrt).then_inc(s_root, 1)
                act.wait_ge(s_xn_v, PRIME + p + 1)
                act.wait_ge(s_xn_p, PRIME + p + 1)
                settle(act)
                for b2 in range(2):
                    act.dma_start(xn_v[ds(p, 1), b2].rearrange("a h c w -> (a h) c w"),
                                  xn_all[64 * b2:64 * b2 + 64, ds(p, 1), C:].rearrange(
                                      "p a (c w) -> p (a c) w", w=W)).then_inc(s_xst, 16)
            act.wait_ge(s_hst, PRIME + 32 * PAIRS)
            act.wait_ge(s_xst, PRIME + 32 * PAIRS)

        @block.tensor
        def _(pe):
            pe.wait_ge(s_w, PRIME + 16 * W_DMAS)
            with pe.Fori(0, PAIRS) as p:
                pe.wait_ge(s_xc, PRIME + (p + 1) * 16)
                settle(pe)
                for j in range(8):
                    if j < 2:
                        pe.wait_ge(s_y, PRIME + p * 8)
                        settle(pe)
                    else:
                        pe.wait_ge(s_y, PRIME + p * 8 + j - 1)
                        settle(pe)
                    nc.tensor.matmul(c1[0:64, j % 2, :], w1[:, :], xc[:, 512 * j:512 * j + 512],
                                     start=True, stop=True).then_inc(s_y1, 1)
                pe.wait_ge(s_y, PRIME + p * 8 + 8)
                pe.wait_ge(s_wd, PRIME + p * 2)
                settle(pe)
                yv = y[:, :].rearrange("r (h w) -> r w h", w=W)
                for w in range(W):
                    for b2 in range(2):
                        k = (w % 32) * K2
                        last = nc.tensor.matmul(c2[64 * b2:64 * b2 + 64, w // 32, k:k + K2], yv[:, w, :],
                                                w2[:, b2, :], start=True, stop=True)
                    if w % 32 == 31:
                        last.then_inc(s_w2, 1)
                pe.wait_ge(s_xn_v, PRIME + p + 1)
                pe.wait_ge(s_xn_p, PRIME + p + 1)
                settle(pe)
                for j in range(8):
                    if j % 2 == 0:
                        pe.wait_ge(s_gr, PRIME + p * 4 + max(j // 2 - 1, 0))
                        settle(pe)
                    for i in range(2):
                        src = xn_all[:, ds(p, 1), 512 * j + C * (1 - i):512 * j + C * (1 - i) + 512]
                        last = nc.tensor.matmul(df[:, j // 2 % 2, 512 * (j % 2):512 * (j % 2) + 512],
                                                shift[:, i, :], src.rearrange("p a n -> p (a n)"),
                                                start=(i == 0), stop=(i == 1))
                    if j % 2:
                        last.then_inc(s_df, 1)

        def convolve(eng, steps, p, a, b, done):
            out = xn_all[:, ds(p, 1), C + a * W:C + b * W].rearrange("p a (c w) -> p (a c) w", w=W)
            for k in range(K2):
                tap = wd[:, k:k + 1, :].to_broadcast([128, b - a, W])
                src = xs[:, k // 3, a:b, k % 3:k % 3 + W]
                if k == 0:
                    steps(eng.tensor_tensor(out, src, tap, ALU.mult))
                else:
                    steps(eng.tensor_tensor(prod[:, a:b, :], src, tap, ALU.mult))
                    last = eng.tensor_tensor(out, out, prod[:, a:b, :], ALU.add)
                    if k < K2 - 1:
                        steps(last)
            last.then_inc(done, 1)

        def channels(p, a, b):
            return xn_all[:, ds(p, 1), C + a * W:C + b * W].rearrange("p a (c w) -> p (a c) w", w=W)

        @block.vector
        def _(dve):
            nc.vector.memset(xn_all[:, :, 0:C], 0.0)
            nc.vector.memset(bn[:, :], 0.0)
            nc.vector.memset(w2[:, :, :], 0.0)
            nc.vector.memset(w1[:, :], 0.0).then_inc(s_set, 1)
            nc.vector.memset(xs[:, :, 0:CD, :], 0.0).then_inc(s_set, 1)
            dve.wait_ge(s_w, PRIME + 16 * W_DMAS)
            STEPS0 = 5
            st = Steps(sem, dve, s_dch, 0)
            nc.vector.tensor_scalar(bn[:, 7:8], bn[:, 4:5], EPS, None, ALU.add).then_inc(s_var, 1)
            dve.wait_ge(s_root, PRIME + 1)
            st(nc.vector.reciprocal(bn[:, 7:8], bn[:, 7:8]))
            st(nc.vector.tensor_tensor(bn[:, 5:6], bn[:, 1:2], bn[:, 7:8], ALU.mult))
            st(nc.vector.tensor_tensor(bn[:, 7:8], bn[:, 0:1], bn[:, 3:4], ALU.subtract))
            st(nc.vector.tensor_tensor(bn[:, 7:8], bn[:, 7:8], bn[:, 5:6], ALU.mult))
            st(nc.vector.tensor_tensor(bn[:, 6:7], bn[:, 7:8], bn[:, 2:3], ALU.add))
            dve.wait_ge(s_set, PRIME + 3)
            nc.vector.tensor_tensor(bn[:, 6:7], bn[:, 6:7], keep["one_rows"][0:64, :], ALU.add
                                    ).then_inc(s_bn, 1)
            assert st.n == STEPS0
            STEPS = 2 * K2 - 2 + 4
            with dve.Fori(0, PAIRS) as p:
                st = Steps(sem, dve, s_dch, p * STEPS + STEPS0)
                dve.wait_ge(s_x, PRIME + (p + 1) * 96)
                dve.wait_ge(s_wd, PRIME + (p + 1) * 2)
                settle(dve)
                convolve(nc.vector, st, p, 0, CD, s_conv_v)
                dve.wait_ge(s_conv_v, PRIME + p + 1)
                dve.wait_ge(s_conv_p, PRIME + p + 1)
                settle(dve)
                st(nc.vector.tensor_reduce(rows[:, 0, :], channels(p, 0, C), AX.X, ALU.add))
                nc.vector.tensor_scalar(rows[:, 1, :], rows[:, 0, :], 1.0 / D, None, ALU.mult
                                        ).then_inc(s_mean, 1)
                dve.wait_ge(s_mean, PRIME + p + 1)
                dve.wait_ge(s_hb, PRIME + p + 1)
                settle(dve)
                nc.vector.tensor_tensor(channels(p, 0, CD), channels(p, 0, CD),
                                        rows[:, 1, 0:CD, None].to_broadcast([128, CD, W]), ALU.subtract
                                        ).then_inc(s_cen_v, 1)
                dve.wait_ge(s_sq, PRIME + p + 1)
                settle(dve)
                st(nc.vector.tensor_reduce(rows[:, 2, :], prod[:, :, :], AX.X, ALU.add))
                nc.vector.tensor_scalar(rows[:, 3, :], rows[:, 2, :], 1.0 / D, EPS, ALU.mult, ALU.add
                                        ).then_inc(s_var, 1)
                dve.wait_ge(s_root, PRIME + p + 2)
                settle(dve)
                nc.vector.reciprocal(rows[:, 3, :], rows[:, 3, :]).then_inc(s_rstd, 1)
                dve.wait_ge(s_rstd, PRIME + p + 1)
                settle(dve)
                nc.vector.tensor_tensor(channels(p, 0, CD), channels(p, 0, CD),
                                        rows[:, 3, 0:CD, None].to_broadcast([128, CD, W]), ALU.mult
                                        ).then_inc(s_xn_v, 1)
                st(nc.vector.tensor_tensor(rows[:, 2, :], rows[:, 2, :], rows[:, 3, :], ALU.mult))
                st(nc.vector.tensor_tensor(std2[:, ds(p, 1), :].rearrange("p a c -> p (a c)"),
                                           rows[:, 2, :], rows[:, 3, :], ALU.mult))
                for j in range(4):
                    dve.wait_ge(s_df, PRIME + p * 4 + j + 1)
                    settle(dve)
                    out = grad[:, ds(p, 1), 16 * j:16 * j + 16].rearrange("p a c -> p (a c)")
                    nc.vector.tensor_reduce(out, df[:, j % 2, :].rearrange("p (c w) -> p c w", w=W), AX.X,
                                            ALU.add, apply_absolute_value=True).then_inc(s_gr, 1)
                assert st.n == STEPS, st.n

        @block.gpsimd
        def _(pool):
            nc.gpsimd.memset(xs[:, :, CD:, :], 0.0)
            nc.gpsimd.memset(keep["one_rows"][:, :], 0.0)
            steps = Steps(sem, pool, s_pch, 0)
            steps(nc.gpsimd.memset(shift[:, :, :], 0.0))
            sel = lambda v, base, step, fill: nc.gpsimd.affine_select(
                out=v, in_=v, compare_op=ALU.not_equal, fill=fill, base=base, pattern=[[step, 128]],
                channel_multiplier=1)
            steps(sel(shift[:, 0, :], 0, -1, 1.0))
            steps(sel(shift[:, 0, :], 1, -1, -1.0))
            steps(nc.gpsimd.memset(shift[:, 1, :], 0.0))
            for b2 in range(2):
                v = shift[:, 1, 64 * b2:64 * b2 + 1]
                steps(nc.gpsimd.affine_select(out=v, in_=v, compare_op=ALU.not_equal, fill=-1.0,
                                              base=-(64 * b2 + 63), pattern=[[0, 1]], channel_multiplier=1))
                v = keep["one_rows"][:, :]
                steps(nc.gpsimd.affine_select(out=v, in_=v, compare_op=ALU.not_equal, fill=1.0,
                                              base=-(32 * b2 + CR), pattern=[[0, 1]], channel_multiplier=1))
            v = shift[:, 0, 64:65]
            steps(nc.gpsimd.affine_select(out=v, in_=v, compare_op=ALU.not_equal, fill=0.0, base=-63,
                                          pattern=[[0, 1]], channel_multiplier=1))
            pool.sem_inc(s_set, 1)
            STEPS0 = steps.n
            pool.wait_ge(s_w, PRIME + 16 * W_DMAS)
            STEPS = 2 * K2 - 2
            with pool.Fori(0, PAIRS) as p:
                st = Steps(sem, pool, s_pch, p * STEPS + STEPS0)
                pool.wait_ge(s_x, PRIME + (p + 1) * 96)
                pool.wait_ge(s_wd, PRIME + (p + 1) * 2)
                settle(pool)
                convolve(nc.gpsimd, st, p, CD, C, s_conv_p)
                pool.wait_ge(s_conv_p, PRIME + p + 1)
                pool.wait_ge(s_conv_v, PRIME + p + 1)
                pool.wait_ge(s_hst, PRIME + 32 * p)
                settle(pool)
                nc.gpsimd.tensor_tensor(hb[:, :, :], channels(p, 0, C), bp[:, None, :].to_broadcast(
                    [128, C, W]), ALU.add).then_inc(s_hb, 1)
                pool.wait_ge(s_mean, PRIME + p + 1)
                pool.wait_ge(s_hb, PRIME + p + 1)
                settle(pool)
                nc.gpsimd.tensor_tensor(channels(p, CD, C), channels(p, CD, C),
                                        rows[:, 1, CD:, None].to_broadcast([128, C - CD, W]), ALU.subtract
                                        ).then_inc(s_cen_p, 1)
                pool.wait_ge(s_rstd, PRIME + p + 1)
                pool.wait_ge(s_sq, PRIME + p + 1)
                settle(pool)
                nc.gpsimd.tensor_tensor(channels(p, CD, C), channels(p, CD, C),
                                        rows[:, 3, CD:, None].to_broadcast([128, C - CD, W]), ALU.mult
                                        ).then_inc(s_xn_p, 1)
                assert st.n == STEPS, st.n


def select_keys(nc, d, keep):
    std2, grad, pos = keep["std2"], keep["grad"], keep["pos"]
    TOTAL = B * NTOK
    MAXIT = NTOK // ITER
    PRE = C // 2
    with ExitStack() as ctx:
        sb = lambda n, s, t=FP32: ctx.enter_context(nc.sbuf_tensor(n, s, t))
        pb = lambda n, s, t=FP32: ctx.enter_context(nc.psum_tensor(n, s, t))
        sem = Sems(nc, ctx)
        settle = sem.settle
        grid = [128, PAIRS, C]
        dens, dev, high, pos_f, tmp = (sb(n, grid) for n in ["dens", "dev", "high", "pos_f", "tmp"])
        at = sb("at", grid)
        pre = [sb(f"pre{i}", [128, PAIRS, PRE + C]) for i in range(2)]
        base = sb("base", [128, PAIRS])
        steps_at = sb("steps_at", [128, MAXIT])
        cnt = sb("cnt", [128, 8, PAIRS])
        some = sb("some", [128, PAIRS, MAXIT])
        niter = sb("niter", [128, PAIRS], I32)
        st = sb("st", [128, 8])
        before, same = sb("before", [128, 128]), sb("same", [128, 128])
        pen_c = sb("pen_c", grid, BF16)
        pen_n = sb("pen_n", [C, PAIRS, 128], BF16)
        neg_pad = sb("neg_pad", [B, 2, PADT], BF16)
        counts = pb("counts", [128, 2, PAIRS])
        turned = pb("turned", [C, PAIRS, 128])
        s_c, s_p, s_v, s_tot, s_cnt, s_ps, s_turn, s_pen = (
            sem(n) for n in ["s_c", "s_p", "s_v", "s_tot", "s_cnt", "s_ps", "s_turn", "s_pen"])
        s_sum, s_pos, s_st, s_var, s_root = (
            sem(n) for n in ["s_sum", "s_pos", "s_st", "s_var", "s_root"])
        ident = keep["ident"]
        sem.prime()
        block = ctx.enter_context(nc.Block())

        @block.gpsimd
        def _(pool):
            step = Steps(sem, pool, s_p, 0)
            aff = nc.gpsimd.affine_select
            nc.gpsimd.memset(neg_pad[:, :, :], NEG)
            nc.gpsimd.memset(before[:, :], 1.0)
            nc.gpsimd.memset(ident[:, :], 0.0)
            step(nc.gpsimd.memset(same[:, :], 0.0))
            for b2 in range(2):
                q = slice(64 * b2, 64 * b2 + 64)
                nc.gpsimd.iota(at[q, :, :], pattern=[[0, PAIRS], [1, C]], base=0, channel_multiplier=C,
                               allow_small_or_imprecise_dtypes=True)
                nc.gpsimd.iota(base[q, :], pattern=[[2 * NTOK, PAIRS]], base=b2 * NTOK,
                               channel_multiplier=0, allow_small_or_imprecise_dtypes=True)
                step(nc.gpsimd.memset(same[q, q], 1.0))
            nc.gpsimd.iota(steps_at[:, :], pattern=[[ITER, MAXIT]], base=0, channel_multiplier=0,
                           allow_small_or_imprecise_dtypes=True)
            step(aff(out=before[:, :], in_=before[:, :], compare_op=ALU.is_gt, fill=0.0, base=0,
                     pattern=[[1, 128]], channel_multiplier=-1))
            step(nc.gpsimd.memset(before[0:64, 64:128], 0.0))
            step(aff(out=ident[:, :], in_=ident[:, :], compare_op=ALU.not_equal, fill=1.0, base=0,
                     pattern=[[-1, 128]], channel_multiplier=1))
            pool.sem_inc(s_c, 1)
            pool.wait_ge(s_sum, PRIME + 1)
            nc.gpsimd.partition_all_reduce(st[:, 1:2], st[:, 0:1], 128, bass.bass_isa.ReduceOp.add
                                           ).then_inc(s_tot, 1)
            pool.wait_ge(s_sum, PRIME + 2)
            nc.gpsimd.partition_all_reduce(st[:, 4:5], st[:, 3:4], 128, bass.bass_isa.ReduceOp.add
                                           ).then_inc(s_tot, 1)

        @block.tensor
        def _(pe):
            pe.wait_ge(s_c, PRIME + 1)
            pe.wait_ge(s_cnt, PRIME + 1)
            nc.tensor.matmul(counts[:, 0, :], before[:, :], cnt[:, 0, :], start=True, stop=True)
            nc.tensor.matmul(counts[:, 1, :], same[:, :], cnt[:, 0, :], start=True, stop=True
                             ).then_inc(s_ps, 1)
            for p in range(PAIRS):
                last = nc.tensor.transpose(turned[:, p, :], high[:, p, :], ident[:, :])
            last.then_inc(s_turn, 1)

        @block.vector
        def _(dve):
            S = Steps(sem, dve, s_v, 0)
            v = nc.vector
            for b2 in range(2):
                v.memset(grad[64 * b2:64 * b2 + 1, :, 0:1], 0.0)
            v.memset(pre[0][:, :, 0:PRE], 0.0)
            S(v.memset(pre[1][:, :, 0:PRE], 0.0))
            S(v.tensor_scalar(dev[:, :, :], std2[:, :, :], 1.0 / (D - 1), None, ALU.mult))
            dve.sem_inc(s_var, 1)
            dve.wait_ge(s_root, PRIME + 1)
            S(v.scalar_tensor_tensor(out=dens[:, :, :], in0=grad[:, :, :], scalar=1.0 / D, in1=dev[:, :, :],
                                     op0=ALU.mult, op1=ALU.add))
            S(v.tensor_scalar(dens[:, :, :], dens[:, :, :], 0.5, None, ALU.mult))
            v.tensor_reduce(st[:, 0:1], dens[:, :, :], AX.XY, ALU.add).then_inc(s_sum, 1)
            dve.wait_ge(s_tot, PRIME + 1)
            S(v.tensor_scalar(st[:, 2:3], st[:, 1:2], 1.0 / TOTAL, None, ALU.mult))
            S(v.tensor_scalar(dev[:, :, :], dens[:, :, :], st[:, 2:3], None, ALU.subtract))
            S(v.tensor_tensor(dev[:, :, :], dev[:, :, :], dev[:, :, :], ALU.mult))
            v.tensor_reduce(st[:, 3:4], dev[:, :, :], AX.XY, ALU.add).then_inc(s_sum, 1)
            dve.wait_ge(s_tot, PRIME + 2)
            S(v.tensor_scalar(st[:, 5:6], st[:, 4:5], 1.0 / (TOTAL - 1), None, ALU.mult))
            dve.sem_inc(s_var, 1)
            dve.wait_ge(s_root, PRIME + 2)
            S(v.scalar_tensor_tensor(out=st[:, 6:7], in0=st[:, 5:6], scalar=0.5, in1=st[:, 2:3],
                                     op0=ALU.mult, op1=ALU.add))
            S(v.tensor_scalar(high[:, :, :], dens[:, :, :], st[:, 6:7], None, ALU.is_gt))
            v.tensor_copy(pre[0][:, :, PRE:], high[:, :, :])
            v.tensor_reduce(cnt[:, 0, :], high[:, :, :], AX.X, ALU.add).then_inc(s_cnt, 1)
            dve.wait_ge(s_cnt, PRIME + 1)
            for i in range(6):
                a, z, n = pre[i % 2], pre[(i + 1) % 2], 1 << i
                S(v.tensor_tensor(z[:, :, PRE:], a[:, :, PRE:], a[:, :, PRE - n:PRE + C - n], ALU.add))
            dve.wait_ge(s_ps, PRIME + 1)
            S(v.tensor_copy(cnt[:, 1:3, :], counts[:, :, :]))
            run = pre[0][:, :, PRE:]
            over_c = lambda i: cnt[:, i, :, None].to_broadcast([128, PAIRS, C])
            S(v.tensor_tensor(run, run, over_c(1), ALU.add))
            S(v.tensor_tensor(pos_f[:, :, :], at[:, :, :], run, ALU.subtract))
            S(v.tensor_tensor(pos_f[:, :, :], pos_f[:, :, :], over_c(2), ALU.add))
            S(v.scalar_tensor_tensor(out=tmp[:, :, :], in0=run, scalar=-1.0, in1=pos_f[:, :, :],
                                     op0=ALU.add, op1=ALU.subtract))
            S(v.tensor_tensor(tmp[:, :, :], tmp[:, :, :], high[:, :, :], ALU.mult))
            S(v.tensor_tensor(pos_f[:, :, :], pos_f[:, :, :], tmp[:, :, :], ALU.add))
            S(v.tensor_tensor(pos_f[:, :, :], pos_f[:, :, :],
                              base[:, :, None].to_broadcast([128, PAIRS, C]), ALU.add))
            v.tensor_copy(pos[:, :], pos_f[:, :, :].rearrange("p a c -> p (a c)")).then_inc(s_pos, 1)
            S(v.tensor_tensor(tmp[:, :, :], at[:, :, :], over_c(2), ALU.is_ge))
            S(v.tensor_scalar(pen_c[:, :, :], tmp[:, :, :], NEG, None, ALU.mult))
            dve.wait_ge(s_turn, PRIME + 1)
            S(v.tensor_scalar(pen_n[:, :, :], turned[:, :, :], NEG, None, ALU.mult))
            S(v.tensor_tensor(some[:, :, :], steps_at[:, None, :].to_broadcast([128, PAIRS, MAXIT]),
                              cnt[:, 2, :, None].to_broadcast([128, PAIRS, MAXIT]), ALU.is_lt))
            S(v.tensor_reduce(cnt[:, 3, :], some[:, :, :], AX.X, ALU.add))
            S(v.tensor_scalar(cnt[:, 4, :], cnt[:, 3, :], 2.0, None, ALU.max))
            v.tensor_copy(niter[:, :], cnt[:, 4, :]).then_inc(s_pen, 1)

        @block.scalar
        def _(act):
            act.wait_ge(s_var, PRIME + 1)
            nc.scalar.activation(dev[:, :, :], dev[:, :, :], ACT.Sqrt).then_inc(s_root, 1)
            act.wait_ge(s_var, PRIME + 2)
            nc.scalar.activation(st[:, 5:6], st[:, 5:6], ACT.Sqrt).then_inc(s_root, 1)

        @block.sync
        def _(sp):
            sp.wait_ge(s_pen, PRIME + 1)
            sp.wait_ge(s_c, PRIME + 1)
            n = 0
            with nc.allow_non_contiguous_dma(reason="a few masks and counts"):
                for b in range(B):
                    p, b2 = b // 2, b % 2
                    q = slice(64 * b2, 64 * b2 + 64)
                    sp.dma_start(d["pen_dram"][b, PADT:PADT + NTOK].rearrange("(c h) -> c h", h=H),
                                 pen_n[:, p, q]).then_inc(s_st, 16)
                    sp.dma_start(d["pen_dram"][B + b, PADT:PADT + NTOK].rearrange("(h c) -> h c", c=C),
                                 pen_c[q, p, :]).then_inc(s_st, 16)
                    n += 2
                for b2 in range(2):
                    sp.dma_start(keep["nit"][0:1, b2::2], niter[64 * b2:64 * b2 + 1, :]).then_inc(s_st, 16)
                    n += 1
                for s in range(2):
                    for k, at0 in enumerate([0, PADT + NTOK]):
                        sp.dma_start(d["pen_dram"][B * s:B * s + B, at0:at0 + PADT], neg_pad[:, k, :]
                                     ).then_inc(s_st, 16)
                        n += 1
            sp.wait_ge(s_st, PRIME + 16 * n)


def project(nc, d, keep):
    T, SUB = 512, 4
    TG = 2
    GT = TG * T
    VW = NH * (HD + 1)
    ident = keep["ident"]
    xn_all, pos = keep["xn_all"], keep["pos"]
    tok_v = [d[n].rearrange("(t s p) w -> t p s w", s=TG * SUB, p=128) for n in ("tok_dram", "tokc_dram")]
    with ExitStack() as ctx:
        sb = lambda n, s, t=FP32: ctx.enter_context(nc.sbuf_tensor(n, s, t))
        pb = lambda n, s, t=FP32: ctx.enter_context(nc.psum_tensor(n, s, t))
        sem = Sems(nc, ctx)
        settle = sem.settle
        tok = sb("tok", [128, 2, TG * SUB, D])
        xt = sb("xt", [D + 1, 2, T])
        wqk = sb("wqk", [D + 1, 128])
        wv = sb("wv", [D + 1, NH, HD + 1])
        scale = sb("scale", [128, 1])
        qk = sb("qk", [128, 2, T])
        rest = sb("rest", [128, 2, T])
        part = sb("part", [128, 2, 3, GT], BF16)
        vt = sb("vt", [128, 2, TG * SUB, VW])
        zero_b = sb("zero_b", [64, 6, PADT], BF16)
        zero_f = sb("zero_f", [PADT, VW])
        tp = pb("tp", [D, 2, SUB, 128])
        qp = pb("qp", [128, 2, T])
        vp = pb("vp", [128, 2, 512])
        s_set, s_w, s_tp, s_xt, s_qp, s_vp, s_qk, s_ve = (
            sem(n) for n in ["s_set", "s_w", "s_tp", "s_xt", "s_qp", "s_vp", "s_qk", "s_ve"])
        s_h, s_r, s_m, s_l, s_z = (
            sem(n) for n in ["s_h", "s_r", "s_m", "s_l", "s_z"])
        s_scat = ctx.enter_context(nc.semaphore("s_scat"))
        s_tok, s_pst, s_vst = ([sem(f"{n}{k}") for k in range(2)] for n in ["s_tok", "s_pst", "s_vst"])
        sem.prime()
        block = ctx.enter_context(nc.Block())
        GROUPS = NTOK // GT
        ITERS = GROUPS // 2
        STORES = [5, 3]

        def tiles(eng, s0, s1):
            with eng.Fori(s0 * ITERS, s1 * ITERS) as i:
                for k in range(2):
                    for c in range(TG):
                        yield (i * 2 + k) * TG + c, i, k, c

        @block.sync
        def _(sp):
            sp.wait_ge(s_set, PRIME + 1)
            with nc.allow_non_contiguous_dma(reason="weights and small pads, once"):
                sp.dma_start(wqk[0:D, :], d["w_qkv"][:, 0:128]).then_inc(s_w, 16)
                sp.dma_start(wv[0:D, :, 0:HD], d["w_qkv"][:, 128:192].rearrange("c (h e) -> c h e", h=NH)
                             ).then_inc(s_w, 16)
                for b in range(B):
                    for at0 in (0, PADT + NTOK):
                        sp.dma_start(d["op_dram"][b, 64:128, :, at0:at0 + PADT], zero_b[:, :, :]).then_inc(s_z, 16)
                        sp.dma_start(d["v_dram"][b, at0:at0 + PADT, :], zero_f[:, :]).then_inc(s_z, 16)
            load = lambda order, t, k: sp.dma_start(tok[:, k, :, :], tok_v[order][ds(t, 1)].rearrange(
                "a p s w -> p (a s) w")).then_inc(s_tok[k], 16)
            for k in range(2):
                load(0, k, k)

            def group(i, k, compact, after):
                n, s, j = i * 2 + k, i // ITERS, (i % ITERS) * 2 + k
                sp.wait_ge(s_tp, PRIME + (n + 1) * TG)
                settle(sp)
                load(*after(n), k)
                dst = lambda r0, r1, i, m: d["op_dram"][ds(s, 1), r0:r1, i:i + m, ds(j * GT + PADT, GT)].rearrange(
                    "a r i n -> (a r) i n")
                store = lambda r0, r1, i, m, src: sp.dma_start(dst(r0, r1, i, m), src).then_inc(s_pst[k], 16)
                twice = lambda a: a.to_broadcast([64, 2, GT])
                sp.wait_ge(s_l, PRIME + (n + 1) * TG)
                settle(sp)
                store(64 if compact else 0, 128, 0, 2, part[64 if compact else 0:128, k, 0:2, :])
                store(64, 128, 2, 2, part[64:128, k, 1:3, :])
                store(64, 128, 4, 2, twice(part[64:128, k, 0:1, :]))
                if not compact:
                    store(0, 64, 2, 2, twice(part[0:64, k, 0:1, :]))
                    store(0, 64, 4, 2, part[0:64, k, 1:3, :])
                sp.wait_ge(s_ve, PRIME + (n + 1) * TG)
                settle(sp)
                sp.dma_start(d["v_dram"][ds(s, 1), ds(j * GT + PADT, GT), :].rearrange(
                    "a (s p) v -> (a p) s v", p=128), vt[:, k, :, :]).then_inc(s_vst[k], 16)

            with sp.Fori(0, B * ITERS - 1) as i:
                for k in range(2):
                    group(i, k, False, lambda n: (0, n + 2))
            sp.wait_ge(s_scat, 16 * PAIRS * C)
            for k in range(2):
                group(B * ITERS - 1, k, False, lambda n: (1, n + 2 - B * GROUPS))
            with sp.Fori(B * ITERS, 2 * B * ITERS) as i:
                for k in range(2):
                    group(i, k, True, lambda n: (1, (n + 2) % (B * GROUPS)))
            for k in range(2):
                sp.wait_ge(s_pst[k], PRIME + 16 * B * ITERS * sum(STORES))
                sp.wait_ge(s_vst[k], PRIME + 16 * 2 * B * ITERS)
                sp.wait_ge(s_tok[k], PRIME + 16 * (2 * B * ITERS + 1))
            sp.wait_ge(s_z, PRIME + 16 * 4 * B)

        @block.gpsimd
        def _(pool):
            for p in range(PAIRS):
                for c in range(C):
                    k = p * C + c
                    pool.indirect_dma_start(
                        out=d["tokc_dram"], out_offset=bass.IndirectOffsetOnAxis(ap=pos[:, k:k + 1], axis=0),
                        in_=xn_all[:, p, C + c * W:C + c * W + W], in_offset=None).then_inc(s_scat, 16)
            pool.wait_ge(s_scat, 16 * PAIRS * C)

        @block.scalar
        def _(act):
            def turned(t, c):
                act.wait_ge(s_tp, PRIME + t + 1)
                act.wait_ge(s_vp, PRIME + t - 1)
                nc.scalar.copy(xt[0:D, c, :], tp[:, c, :, :].rearrange("c s p -> c (s p)")
                               ).then_inc(s_xt, 1)

            turned(0, 0)
            for compact in (False, True):
                for t, i, k, c in tiles(act, B * compact, B * compact + B):
                    turned(t + 1, 1 - c)
                    act.wait_ge(s_r, PRIME + t - 1)
                    act.wait_ge(s_qp, PRIME + t + 1)
                    nc.scalar.activation(qk[:, c, :], qp[:, c, :], ACT.Copy, scale=scale[:, 0:1]
                                         ).then_inc(s_qk, 1)
                    before = B * ITERS * (STORES[0] - STORES[1]) if compact else 0
                    act.wait_ge(s_pst[k], i * (16 * STORES[compact]) + (PRIME + 16 * before))
                    nc.scalar.activation(part[:, k, 0, T * c:T * c + T], qp[:, c, :], ACT.Copy,
                                         scale=scale[:, 0:1]).then_inc(s_h, 1)
                    act.wait_ge(s_vst[k], PRIME + i * 16)
                    act.wait_ge(s_vp, PRIME + t + 1)
                    nc.scalar.copy(vt[:, k, SUB * c:SUB * c + SUB, :], vp[:, c, 0:SUB * VW].rearrange(
                        "p (s v) -> p s v", s=SUB)).then_inc(s_ve, 1)

        @block.tensor
        def _(pe):
            pe.wait_ge(s_w, PRIME + 32)

            def turn(t, i, k, c):
                pe.wait_ge(s_tok[k], PRIME + i * 16 + 16)
                pe.wait_ge(s_xt, PRIME + t - 1)
                settle(pe)
                for q in range(SUB):
                    last = nc.tensor.transpose(tp[:, c, q, :], tok[:, k, SUB * c + q, :], ident[:, :])
                last.then_inc(s_tp, 1)

            turn(0, 0, 0, 0)
            for t, i, k, c in tiles(pe, 0, 2 * B):
                if c == 0:
                    turn(t + 1, i, k, 1)
                else:
                    turn(t + 1, i + k, 1 - k, 0)
                pe.wait_ge(s_h, PRIME + t - 1)
                pe.wait_ge(s_xt, PRIME + t + 1)
                nc.tensor.matmul(qp[:, c, :], wqk[:, :], xt[:, c, :], start=True, stop=True
                                 ).then_inc(s_qp, 1)
                pe.wait_ge(s_ve, PRIME + t - 1)
                for q in range(SUB):
                    last = nc.tensor.matmul(vp[:, c, VW * q:VW * q + VW], xt[:, c, 128 * q:128 * q + 128],
                                            wv[:, :, :].rearrange("c h e -> c (h e)"), start=True, stop=True)
                last.then_inc(s_vp, 1)

        @block.vector
        def _(dve):
            v = nc.vector
            v.memset(xt[:, :, :], 1.0)
            v.memset(wqk[:, :], 0.0)
            v.memset(wv[0:D, :, :], 0.0)
            v.memset(wv[D:D + 1, :, 0:HD], 0.0)
            v.memset(zero_b[:, :, :], 0.0)
            v.memset(zero_f[:, :], 0.0)
            v.memset(scale[0:64, :], float(HD) ** -0.5)
            v.memset(scale[64:128, :], 1.0)
            v.memset(wv[D:D + 1, :, HD:], 1.0).then_inc(s_set, 1)
            for t, i, k, c in tiles(dve, 0, 2 * B):
                piece = lambda m: part[:, k, m, T * c:T * c + T]
                dve.wait_ge(s_qk, PRIME + t + 1)
                dve.wait_ge(s_h, PRIME + t + 1)
                v.tensor_tensor(rest[:, c, :], qk[:, c, :], piece(0), ALU.subtract).then_inc(s_r, 1)
                dve.wait_ge(s_r, PRIME + t + 1)
                v.tensor_copy(piece(1), rest[:, c, :]).then_inc(s_m, 1)
                dve.wait_ge(s_m, PRIME + t + 1)
                v.tensor_tensor(piece(2), rest[:, c, :], piece(1), ALU.subtract).then_inc(s_l, 1)


def attend(nc, d, keep):
    G, HG = 2, NH // 2
    Q = 512
    NQ = NTOK // Q
    QW, KW = 64, 96
    NW = Q // QW
    LW = 128 + 2 * WINDOW
    KL_W = Q + 2 * PADT
    ROWS_MAX, ROWS = 97, 103
    CH = 128
    VW = HD + 1
    HROWS = 6 * HD
    MAXIT = NTOK // ITER
    GRP_S, GRP_M = 4, 8
    nit, ident = keep["nit"], keep["ident"]
    tok = lambda a: a.rearrange("(t s p) w -> t p s w", s=Q // 128, p=128)
    h_v, h1_v = tok(d["h_dram"].rearrange("b n w -> (b n) w")), tok(d["h1_dram"])
    v_rows = d["v_dram"].rearrange("s n v -> (s n) v")
    with ExitStack() as ctx:
        sb = lambda n, s, t=FP32: ctx.enter_context(nc.sbuf_tensor("a_" + n, s, t))
        pb = lambda n, s, t=FP32: ctx.enter_context(nc.psum_tensor("a_" + n, s, t))
        sem = Sems(nc, ctx)
        settle = sem.settle
        kc = sb("kc", [128, NH, NTOK], BF16)
        vc = sb("vc", [128, 2 * (NTOK // CH), NH * VW])
        qm = sb("qm", [128, G, 2, Q], BF16)
        qe = sb("qe", [128, G, 2, Q], BF16)
        kl = sb("kl", [128, G, HG, KL_W], BF16)
        vl = sb("vl", [KW, NW, HG * VW])
        vs = sb("vs", [128, 2, HG * VW])
        probs = sb("probs", [128, 4, 2 * Q])
        mx = sb("mx", [128, MAXIT + 1, HG * 4])
        nm = sb("nm", [128, 2, 2, 4])
        rest = sb("rest", [128, 2, 2, 4])
        mt = sb("mt", [128, 4, 2, 7], BF16)
        ot = sb("ot", [128, Q])
        inv = sb("inv", [128, 4, HG])
        on = sb("on", [128, 4, D])
        ont = sb("ont", [D, Q])
        wp = sb("wp", [D, D])
        ht = sb("ht", [128, 4, D])
        h1 = sb("h1", [128, 4, D])
        ones3 = sb("ones3", [3, NTOK], BF16)
        one_row = sb("one_row", [1, 2 * Q], BF16)
        identb = sb("identb", [128, 128], BF16)
        band_q = sb("band_q", [128, 2, LW], BF16)
        band_k = sb("band_k", [128, NW, QW], BF16)
        zeros = sb("zeros4", [128, 32])
        ps_s = pb("ps_s", [128, 2, 2 * Q])
        ps_m = pb("ps_m", [128, 2, 512])
        ps_o = pb("ps_o", [128, Q])
        aux = pb("aux", [128, 512])
        aux_b = aux[:, :].bitcast(BF16)
        (s_set, s_cst, s_kc, s_h, s_vl, s_st) = (sem(n) for n in [
            "s_set", "s_cst", "s_kc", "s_h", "s_vl", "s_st"])
        s_keys = [sem(f"s_keys{g}") for g in range(G)]
        s_qm, s_qe, s_kl = ([sem(f"{n}{g}") for g in range(G)] for n in ["s_qm", "s_qe", "s_kl"])
        (s_sc, s_pr, s_pv, s_mx, s_mr, s_vs) = (sem(n) for n in [
            "s_sc", "s_pr", "s_pv", "s_mx", "s_mr", "s_vs"])
        (s_fm, s_mts, s_mt, s_row, s_loc, s_pvl, s_ot, s_r, s_inv, s_on, s_ont, s_onc, s_pj, s_fin, s_mch, s_mlm,
         s_gset) = (sem(n) for n in ["s_fm", "s_mts", "s_mt", "s_row", "s_loc", "s_pvl", "s_ot", "s_r", "s_inv",
                                     "s_on", "s_ont", "s_onc", "s_pj", "s_fin", "s_mch", "s_mlm", "s_gset"])
        sem.prime()
        block = ctx.enter_context(nc.Block())
        UNITS = B * NQ * G
        KCH = 1024
        VCH = 512
        KEYS_DMAS = [3 + KCH // VCH, 3]
        Q_DMAS, KL_DMAS, VL_DMAS = 1, 3, 2
        CONSTANTS = 6 * NH + G + 1

        class Count:

            def __init__(self, eng):
                self.eng = eng
                self.reg, self.reg_keys = eng.alloc_register("iterations"), eng.alloc_register("key_blocks")
                eng.reg_mov(self.reg, 0)
                eng.reg_mov(self.reg_keys, 0)

            def batch(self, b):
                self.b = b
                self.n = self.eng.value_load(nit[0:1, ds(b, 1)], min_val=2, max_val=MAXIT)
                self.unit()

            def unit(self):
                self.base = self.eng.snap(self.reg)
                self.keys = self.eng.snap(self.reg_keys)

            def done(self):
                self.eng.reg_add(self.reg, self.reg, self.n + 1)
                self.eng.reg_add(self.reg_keys, self.reg_keys, self.n)

        def schedule(eng, count, lead, unit):
            with eng.Fori(0, B) as b:
                count.batch(b)
                lead(b)
                with eng.Fori(0, NQ - 1) as q:
                    for g in range(G):
                        count.unit()
                        unit(b * NQ + q, g, True)
                        count.done()
                for g in range(G):
                    count.unit()
                    unit(b * NQ + (NQ - 1), g, g == 0)
                    count.done()

        def over_keys(eng, count, body):
            with eng.Fori(0, count.n - 1) as it:
                body(it, False)
            body(count.n - 1, True)

        @block.sync
        def _(sp):
            def keys_of(dst, stream, g, n0, n, s):
                src = d["op_dram"][ds(stream, 1), 64 + 32 * g:96 + 32 * g, :, ds(n0, n)].rearrange(
                    "a (j hh e) i n -> hh (a e i) j n", j=2, hh=2)
                for hh in range(2):
                    sp.dma_start(dst.rearrange("p (j hh) n -> p hh j n", hh=2)[HROWS * hh:HROWS * hh + HROWS, hh],
                                 src[hh]).then_inc(s, 16)

            def load_q(dst, T, g, s):
                sp.dma_start(dst[0:2 * HROWS, g, :, :], d["op_dram"][
                    ds(T // NQ, 1), 32 * g:32 * g + 32, :, ds((T % NQ) * Q + PADT, Q)].rearrange(
                    "a (j r) i n -> (a r i) j n", j=2)).then_inc(s, 16)

            def load_kl(T, g):
                keys_of(kl[:, g, :, :], T // NQ, g, (T % NQ) * Q, KL_W, s_kl[g])
                sp.dma_start(kl[96:97, g, :, :], d["pen_dram"][ds(T // NQ, 1), ds((T % NQ) * Q, KL_W)][
                    :, None, :].to_broadcast([1, HG, KL_W])).then_inc(s_kl[g], 16)

            def load_vl(T, g):
                for p0, p1 in ((0, QW), (QW, KW)):
                    src = v_rows[ds((T // NQ) * TP + (T % NQ) * Q + p0, Q), :].rearrange(
                        "(w p) v -> p w v", p=QW)[0:p1 - p0, :, HG * VW * g:HG * VW * (g + 1)]
                    sp.dma_start(vl[p0:p1, :, :], src).then_inc(s_vl, 16)

            sp.wait_ge(s_set, PRIME + 2)
            n = 0
            for h in range(NH):
                for i in range(3):
                    r = 97 + 2 * i + h % 2
                    sp.dma_start(kc[r:r + 1, h, :], ones3[0:1, :]).then_inc(s_cst, 16)
                    sp.dma_start(kl[r:r + 1, h // HG, h % HG, :], ones3[0:1, 0:KL_W]).then_inc(s_cst, 16)
                    n += 2
            for g in range(G):
                sp.dma_start(qm[96:97, g, :, :], one_row[0:1, :]).then_inc(s_cst, 16)
                n += 1
            sp.dma_start(wp[:, :], d["w_proj"]).then_inc(s_cst, 16)
            n += 1
            assert n == CONSTANTS
            for g in range(G):
                load_kl(0, g)
                load_q(qm, 0, g, s_qm[g])
            load_q(qe, 0, 0, s_qe[0])
            load_vl(0, 0)

            loaded = sp.alloc_register("key_loads")
            sp.reg_mov(loaded, PRIME)

            def load_keys(b, g):
                n = sp.value_load(nit[0:1, ds(b, 1)], min_val=2, max_val=MAXIT)
                chunks = sp.snap((n + (KCH // ITER - 1)) // (KCH // ITER))
                with sp.Fori(0, chunks) as c:
                    at0 = sp.snap(c * KCH)
                    keys_of(kc[:, HG * g:HG * g + HG, ds(at0, KCH)], b + B, g, at0 + PADT, KCH, s_kc)
                    sp.dma_start(kc[96:97, HG * g:HG * g + HG, ds(at0, KCH)], d["pen_dram"][
                        ds(b + B, 1), ds(at0 + PADT, KCH)][:, None, :].to_broadcast([1, HG, KCH])).then_inc(s_kc, 16)
                    if g == 0:
                        for i in range(KCH // VCH):
                            sp.dma_start(vc[:, ds((b % 2) * (NTOK // CH) + c * (KCH // CH) + i * (VCH // CH), VCH // CH), :],
                                         d["v_dram"][ds(b + B, 1), ds(at0 + (PADT + VCH * i), VCH), :].rearrange(
                                         "a (c p) v -> (a p) c v", p=CH)).then_inc(s_kc, 16)
                sp.reg_add(loaded, loaded, chunks * (16 * KEYS_DMAS[g]))

            def keys_there(g):
                sp.wait_ge(s_kc, sp.snap(loaded))
                settle(sp)
                sp.sem_inc(s_keys[g], 1)

            def unit(T, g, last):
                U = T * G + g
                if not last:
                    sp.wait_ge(s_loc, PRIME + U + 1)
                    settle(sp)
                    load_kl(T + 1, g)
                    sp.wait_ge(s_fm, PRIME + U + 1)
                    settle(sp)
                    load_q(qm, T + 1, g, s_qm[g])
                if not (last and g == 1):
                    sp.wait_ge(s_ot, PRIME + U)
                    settle(sp)
                    load_q(qe, T + g, 1 - g, s_qe[1 - g])
                    sp.wait_ge(s_pvl, PRIME + U + 1)
                    settle(sp)
                    load_vl(T + g, 1 - g)
                if g == 0:
                    sp.wait_ge(s_fin, PRIME + T + 1)
                    settle(sp)
                    sp.dma_start(h1_v[ds((T + (B * NQ - 1)) % (B * NQ), 1)].rearrange("a p s w -> p (a s) w"),
                                 h1[:, :, :]).then_inc(s_st, 16)
                    sp.dma_start(ht[:, :, :], h_v[ds(T, 1)].rearrange("a p s w -> p (a s) w")
                                 ).then_inc(s_h, 16)

            for g in range(G):
                load_keys(0, g)
                keys_there(g)
            with sp.Fori(0, B - 1) as b:
                with sp.Fori(0, NQ - 1) as q:
                    for g in range(G):
                        unit(b * NQ + q, g, False)
                T = b * NQ + (NQ - 1)
                unit(T, 0, False)
                sp.wait_ge(s_ot, PRIME + T * G + 1)
                settle(sp)
                load_keys(b + 1, 0)
                unit(T, 1, False)
                keys_there(0)
                sp.wait_ge(s_ot, PRIME + T * G + 2)
                settle(sp)
                load_keys(b + 1, 1)
                keys_there(1)
            with sp.Fori(0, NQ - 1) as q:
                for g in range(G):
                    unit((B - 1) * NQ + q, g, False)
            for g in range(G):
                unit(B * NQ - 1, g, True)
            sp.wait_ge(s_fin, PRIME + B * NQ + 1)
            sp.wait_ge(s_st, PRIME + 16 * B * NQ)
            sp.dma_start(h1_v[B * NQ - 1], h1[:, :, :]).then_inc(s_st, 16)
            sp.wait_ge(s_st, PRIME + 16 * (B * NQ + 1))

        @block.tensor
        def _(pe):
            mm = nc.tensor.matmul
            count = Count(pe)

            def maxima_windows(T, g, base, k0, k1):
                pe.wait_ge(s_kl[g], PRIME + (T + 1) * (16 * KL_DMAS))
                pe.wait_ge(s_qm[g], PRIME + (T + 1) * (16 * Q_DMAS))
                for k in range(k0, k1):
                    h, j = k // 2, k // 4
                    pe.wait_ge(s_mr, PRIME + base * GRP_M + k - 1)
                    bank = ps_m[:, k % 2, 0:2 * LW]
                    mm(bank, identb[:, :], band_q[:, :, :].rearrange("p a n -> p (a n)"), start=True, stop=False,
                       skip_group_check=True)
                    for i in range(2):
                        sub = 2 * (k % 2) + i
                        last = mm(ps_m[:, k % 2, LW * i:LW * i + LW], qm[0:ROWS_MAX, g, j, 128 * sub:128 * sub + 128],
                                  kl[0:ROWS_MAX, g, h, 128 * sub:128 * sub + LW], start=False, stop=(i == 1),
                                  skip_group_check=True)
                    last.then_inc(s_mx, 1)

            def maxima_block(g, base, it, k):
                h, j = k // 2, k // 4
                pe.wait_ge(s_mr, PRIME + (base + 1 + it) * GRP_M + k - 1)
                for i in range(2):
                    sub = 2 * (k % 2) + i
                    last = mm(ps_m[:, k % 2, ITER * i:ITER * i + ITER], qm[0:ROWS_MAX, g, j, 128 * sub:128 * sub + 128],
                              kc[0:ROWS_MAX, HG * g + h, ds(it * ITER, ITER)], start=True, stop=True)
                last.then_inc(s_mx, 1)

            def lead(b):
                pe.wait_ge(s_keys[0], PRIME + b + 1)
                maxima_windows(b * NQ, 0, count.base, 0, GRP_M)
                body = lambda it, last: [maxima_block(0, count.base, it, k) for k in range(GRP_M)]
                over_keys(pe, count, body)

            def turn_sums():
                for sub in range(4):
                    last = nc.tensor.transpose(aux[:, 128 * sub:128 * sub + 128], ot[:, 128 * sub:128 * sub + 128],
                                               ident[:, :])
                last.then_inc(s_r, 1)

            def turn_outputs():
                for sub in range(4):
                    last = nc.tensor.transpose(aux[0:D, 128 * sub:128 * sub + 128], on[:, sub, :], ident[:, :])
                last.then_inc(s_ont, 1)

            def projection():
                for sub in range(4):
                    last = mm(aux[:, D * sub:D * sub + D], ont[:, 128 * sub:128 * sub + 128], wp[:, :],
                              start=True, stop=True)
                last.then_inc(s_pj, 1)

            def unit(T, g, ahead):
                U = T * G + g
                base, after = count.base, count.base + count.n + 1
                if ahead:
                    maxima_windows(T + g, 1 - g, after, 0, 6)
                pe.wait_ge(s_on, PRIME + U)
                pe.wait_ge(s_fin, PRIME + T + g)
                pe.wait_ge(s_mts, PRIME + U + 1)
                for j in range(2):
                    for sub in range(4):
                        last = nc.tensor.transpose(aux_b[96:103, 512 * j + 128 * sub:512 * j + 128 * sub + 128],
                                                   mt[:, sub, j, :], identb[:, :])
                last.then_inc(s_mt, 1)
                if ahead:
                    maxima_windows(T + g, 1 - g, after, 6, GRP_M)
                pe.wait_ge(s_qe[g], PRIME + (T + 1) * (16 * Q_DMAS))
                for jj in range(2):
                    pe.wait_ge(s_pr, PRIME + base * GRP_S - 1 + jj)
                    pe.wait_ge(s_row, PRIME + U * 2 + jj + 1)
                    for hh in range(2):
                        h = 2 * jj + hh
                        mm(ps_s[0:KW, jj, Q * hh:Q * hh + Q], identb[:, 0:KW],
                           band_k[:, :, :].rearrange("p a n -> p (a n)"), start=True, stop=False,
                           skip_group_check=True)
                        for w in range(NW):
                            at0 = Q * hh + QW * w
                            last = mm(ps_s[0:KW, jj, at0:at0 + QW], kl[0:ROWS, g, h, QW * w:QW * w + KW],
                                      qe[0:ROWS, g, jj, QW * w:QW * w + QW], start=False, stop=(w == NW - 1),
                                      skip_group_check=True)
                    last.then_inc(s_sc, 2)
                pe.wait_ge(s_ot, PRIME + U)
                turn_sums()
                pe.wait_ge(s_vl, PRIME + (U + 1) * (16 * VL_DMAS))
                for jj in range(2):
                    pe.wait_ge(s_pr, PRIME + base * GRP_S + 2 * jj + 2)
                    for hh in range(2):
                        h = 2 * jj + hh
                        for w in range(NW):
                            last = mm(ps_o[32 * h:32 * h + VW, QW * w:QW * w + QW], vl[:, w, VW * h:VW * h + VW],
                                      probs[0:KW, 2 + jj, Q * hh + QW * w:Q * hh + QW * w + QW],
                                      start=(w == 0), stop=False, skip_group_check=True)
                    last.then_inc(s_pv, 2)

                def scores(it, k):
                    jj = k % 2
                    pe.wait_ge(s_pr, PRIME + (base + 1 + it) * GRP_S + k - 1)
                    for hh in range(2):
                        last = mm(ps_s[:, k % 2, Q * hh:Q * hh + Q],
                                  kc[0:ROWS, HG * g + 2 * jj + hh, ds(it * ITER + CH * (k // 2), CH)],
                                  qe[0:ROWS, g, jj, :], start=True, stop=True)
                    last.then_inc(s_sc, 1)

                def products(k, n0, n1, end):
                    for hh in range(2):
                        h = 2 * (k % 2) + hh
                        last = mm(ps_o[32 * h:32 * h + VW, n0:n1], vs[:, k // 2, VW * h:VW * h + VW],
                                  probs[:, k, Q * hh + n0:Q * hh + n1], start=False, stop=end,
                                  skip_group_check=True)
                    return last

                def values(it, k, end):
                    if k % 2 == 0:
                        pe.wait_ge(s_vs, PRIME + (count.keys + it) * 2 + k // 2 + 1)
                        pe.wait_ge(s_pr, PRIME + (base + 1 + it) * GRP_S + k + 1)
                        products(k, 0, Q // 2, end)
                    else:
                        products(k - 1, Q // 2, Q, end).then_inc(s_pv, 1)
                        pe.wait_ge(s_pr, PRIME + (base + 1 + it) * GRP_S + k + 1)
                        products(k, 0, Q, end).then_inc(s_pv, 1)

                def body(it, end):
                    for k in range(GRP_S):
                        if end and g == 0 and k == 2:
                            pe.wait_ge(s_onc, PRIME + T + 1)
                            projection()
                        if ahead:
                            maxima_block(1 - g, after, it, 2 * k)
                        if not (end and k == GRP_S - 1):
                            scores(it + (k + 1) // GRP_S, (k + 1) % GRP_S)
                        if ahead:
                            maxima_block(1 - g, after, it, 2 * k + 1)
                        values(it, k, end and k >= 2)

                scores(0, 0)
                if g == 0:
                    pe.wait_ge(s_keys[1], PRIME + count.b + 1)
                    settle(pe)
                with pe.Fori(0, count.n - 1) as it:
                    body(it, False)
                if g == 0:
                    pe.wait_ge(s_on, PRIME + U + 1)
                    settle(pe)
                    turn_outputs()
                body(count.n - 1, True)

            pe.wait_ge(s_cst, PRIME + 16 * CONSTANTS)
            pe.wait_ge(s_set, PRIME + 2)
            for h in range(HG):
                mm(ps_o[32 * h:32 * h + 32, :], zeros[:, :], ot[:, :], start=True, stop=True)
            schedule(pe, count, lead, unit)
            pe.wait_ge(s_ot, PRIME + UNITS)
            pe.wait_ge(s_fin, PRIME + B * NQ)
            pe.wait_ge(s_on, PRIME + UNITS)
            turn_sums()
            pe.wait_ge(s_on, PRIME + UNITS + 1)
            turn_outputs()
            pe.wait_ge(s_onc, PRIME + B * NQ + 1)
            projection()

        @block.scalar
        def _(act):
            count = Count(act)

            def unit(T, g, ahead):
                U = T * G + g
                base = count.base
                act.wait_ge(s_mt, PRIME + U + 1)
                for j in range(2):
                    nc.scalar.copy(qe[96:103, g, j, :], aux_b[96:103, 512 * j:512 * j + 512]).then_inc(s_row, 1)
                for jj in range(2):
                    act.wait_ge(s_sc, PRIME + base * GRP_S + 2 * jj + 2)
                    if jj == 1:
                        act.sem_inc(s_loc, 1)
                    act.wait_ge(s_pv, PRIME + base * GRP_S - 1 + jj)
                    nc.scalar.activation(probs[0:KW, 2 + jj, :], ps_s[0:KW, jj, :], ACT.Exp).then_inc(s_pr, 2)

                def body(it, end):
                    for k in range(GRP_S):
                        act.wait_ge(s_sc, PRIME + (base + 1 + it) * GRP_S + k + 1)
                        act.wait_ge(s_pv, PRIME + (base + 1 + it) * GRP_S - 3 + k)
                        nc.scalar.activation(probs[:, k, :], ps_s[:, k % 2, :], ACT.Exp).then_inc(s_pr, 1)

                with act.Fori(0, count.n - 1) as it:
                    body(it, False)
                if g == 0:
                    act.wait_ge(s_pj, PRIME + T)
                    act.wait_ge(s_ont, PRIME + T + 1)
                    nc.scalar.copy(ont[:, :], aux[0:D, :]).then_inc(s_onc, 1)
                body(count.n - 1, True)
                act.wait_ge(s_r, PRIME + U + 1)
                act.wait_ge(s_pv, PRIME + (base + 1 + count.n) * GRP_S)
                nc.scalar.copy(ot[:, :], ps_o[:, :]).then_inc(s_ot, 1)

            schedule(act, count, lambda b: None, unit)
            act.wait_ge(s_ont, PRIME + B * NQ + 1)
            nc.scalar.copy(ont[:, :], aux[0:D, :]).then_inc(s_onc, 1)

        @block.vector
        def _(dve):
            v = nc.vector
            v.memset(kc[:, 0:4, :].bitcast(U32), 0)
            v.memset(kl[:, :, :, :].bitcast(U32), 0)
            v.memset(ones3[:, :], 1.0)
            v.memset(one_row[:, :], 1.0)
            v.memset(mt[:, :, :, 0:1], 1.0)
            v.memset(ht[:, :, :], 0.0)
            v.memset(on[:, :, :], 0.0)
            v.memset(ot[:, :], 1.0)
            v.memset(zeros[:, :], 0.0)
            v.tensor_copy(identb[:, :], ident[:, :]).then_inc(s_set, 1)
            count = Count(dve)

            def maxima_windows(base, k0, k1):
                for k in range(k0, k1):
                    dve.wait_ge(s_mx, PRIME + base * GRP_M + k + 1)
                    v.tensor_reduce(mx[:, 0, 2 * k:2 * k + 2], ps_m[:, k % 2, 0:2 * LW].rearrange(
                        "p (a n) -> p a n", a=2), AX.X, ALU.max).then_inc(s_mr, 1)

            def maxima_block(base, it, k0=0, k1=GRP_M):
                for k in range(k0, k1):
                    dve.wait_ge(s_mx, PRIME + (base + 1 + it) * GRP_M + k + 1)
                    settle(dve)
                    v.tensor_reduce(mx[:, ds(it + 1, 1), 2 * k:2 * k + 2], ps_m[:, k % 2, :].rearrange(
                        "p (a n) -> p a n", a=2), AX.X, ALU.max).then_inc(s_mr, 1)

            def lead(b):
                v.memset(mx[:, :, :], -3.0e38).then_inc(s_mlm, 1)
                dve.wait_ge(s_mlm, PRIME + b + 1)
                settle(dve)
                maxima_windows(count.base, 0, GRP_M)
                over_keys(dve, count, lambda it, end: maxima_block(count.base, it))

            def normalise(U, T, g):
                sums = aux[:, :].rearrange("p (s h r) -> p s h r", s=4, h=HG)
                dve.wait_ge(s_r, PRIME + U + 1)
                v.reciprocal(inv[:, :, :], sums[:, :, :, HD]).then_inc(s_inv, 1)
                dve.wait_ge(s_ont, PRIME + T + g)
                dve.wait_ge(s_inv, PRIME + U + 1)
                v.tensor_tensor(on[:, :, 32 * (1 - g):32 * (1 - g) + 32].rearrange("p s (h e) -> p s h e", h=HG),
                                sums[:, :, :, 0:HD], inv[:, :, :, None].to_broadcast([128, 4, HG, HD]), ALU.mult
                                ).then_inc(s_on, 1)

            def unit(T, g, ahead):
                U = T * G + g
                after = count.base + count.n + 1
                dve.wait_ge(s_mr, PRIME + after * GRP_M)
                v.tensor_reduce(nm[:, :, :, :].rearrange("p j h s -> p (j h s)"), mx[:, :, :].rearrange(
                    "p i k -> p k i"), AX.X, ALU.max, negate=True).then_inc(s_fm, 1)
                part = lambda i: mt[:, :, :, 1 + 2 * i:3 + 2 * i].rearrange("p s j h -> p j h s")
                dve.wait_ge(s_mt, PRIME + U)
                dve.wait_ge(s_fm, PRIME + U + 1)
                v.tensor_copy(part(0), nm[:, :, :, :]).then_inc(s_mch, 1)
                if ahead:
                    maxima_windows(after, 0, 1)
                dve.wait_ge(s_mch, PRIME + U * 4 + 1)
                v.tensor_tensor(rest[:, :, :, :], nm[:, :, :, :], part(0), ALU.subtract).then_inc(s_mch, 1)
                if ahead:
                    maxima_windows(after, 1, 2)
                dve.wait_ge(s_mch, PRIME + U * 4 + 2)
                v.tensor_copy(part(1), rest[:, :, :, :]).then_inc(s_mch, 1)
                if ahead:
                    maxima_windows(after, 2, 3)
                dve.wait_ge(s_mch, PRIME + U * 4 + 3)
                v.tensor_tensor(rest[:, :, :, :], rest[:, :, :, :], part(1), ALU.subtract).then_inc(s_mch, 1)
                if ahead:
                    maxima_windows(after, 3, 4)
                dve.wait_ge(s_mch, PRIME + U * 4 + 4)
                v.tensor_copy(part(2), rest[:, :, :, :]).then_inc(s_mts, 1)
                if ahead:
                    maxima_windows(after, 4, GRP_M)
                normalise(U, T, g)
                if ahead:
                    with dve.Fori(0, count.n - 1) as it:
                        maxima_block(after, it)
                    maxima_block(after, count.n - 1, 0, GRP_M // 2)
                if g == 0:
                    dve.wait_ge(s_h, PRIME + 16 * T)
                    dve.wait_ge(s_st, PRIME + 16 * T)
                    dve.wait_ge(s_pj, PRIME + T + 1)
                    v.tensor_tensor(h1[:, :, :], ht[:, :, :], aux[:, 0:4 * D].rearrange(
                        "p (s w) -> p s w", s=4), ALU.add).then_inc(s_fin, 1)
                if ahead:
                    maxima_block(after, count.n - 1, GRP_M // 2, GRP_M)

            schedule(dve, count, lead, unit)
            normalise(UNITS, B * NQ, 0)
            dve.wait_ge(s_pj, PRIME + B * NQ + 1)
            dve.wait_ge(s_h, PRIME + 16 * B * NQ)
            dve.wait_ge(s_st, PRIME + 16 * B * NQ)
            v.tensor_tensor(h1[:, :, :], ht[:, :, :], aux[:, 0:4 * D].rearrange(
                "p (s w) -> p s w", s=4), ALU.add).then_inc(s_fin, 1)

        @block.gpsimd
        def _(pool):
            g_ = nc.gpsimd
            g_.memset(kc[:, 4:8, :].bitcast(U32), 0)
            g_.memset(band_q[:, :, :], 0.0)
            g_.memset(band_k[:, :, :], 0.0).then_inc(s_gset, 1)
            pool.wait_ge(s_gset, PRIME + 1)
            aff = lambda t, base, pat, cm, fill, op: g_.affine_select(
                out=t, in_=t, compare_op=op, fill=fill, base=base, pattern=pat, channel_multiplier=cm)
            aff(band_q[:, :, :], 0, [[0, 2], [1, LW]], -1, NEG, ALU.is_gt)
            aff(band_k[:, :, :], 0, [[0, NW], [-1, QW]], 1, NEG, ALU.is_gt).then_inc(s_gset, 1)
            pool.wait_ge(s_gset, PRIME + 2)
            aff(band_q[:, :, :], 2 * WINDOW, [[0, 2], [-1, LW]], 1, NEG, ALU.is_gt)
            aff(band_k[:, :, :], 2 * WINDOW, [[0, NW], [1, QW]], -1, NEG, ALU.is_gt).then_inc(s_set, 1)
            count = Count(pool)

            def lead(b):
                pool.wait_ge(s_keys[0], PRIME + b + 1)
                settle(pool)

            def unit(T, g, ahead):
                U = T * G + g
                base = count.base
                pool.wait_ge(s_pv, PRIME + (base + 1) * GRP_S)
                settle(pool)
                pool.sem_inc(s_pvl, 1)

                def stage(it):
                    for c in range(2):
                        pool.wait_ge(s_pv, PRIME + (base + 1 + it) * GRP_S - 2 + 2 * c)
                        settle(pool)
                        g_.tensor_copy(vs[:, c, :], vc[:, ds((count.b % 2) * (NTOK // CH) + it * 2 + c, 1), HG * VW * g:HG * VW * (g + 1)]
                                       .rearrange("p a v -> p (a v)")).then_inc(s_vs, 1)

                stage(0)
                with pool.Fori(1, count.n) as it:
                    stage(it)

            schedule(pool, count, lead, unit)


TOK_BLOCK = 8
BLOCKS = B * NTOK // (128 * TOK_BLOCK)
QUADS = TOK_BLOCK // 2


def route(nc, d, keep):
    GB = 4
    GS = GB * TOK_BLOCK
    GROUPS, PER = BLOCKS // GB, 2
    CS = 2 * GS
    CHUNKS = BLOCKS * TOK_BLOCK // CS
    N = 128 * QUADS
    ident, xt, rw = keep["ident"], keep["xt_all"], keep["rw"]
    h_v = d["h1_dram"].rearrange("(t p s) w -> t p s w", s=TOK_BLOCK, p=128)
    with ExitStack() as ctx:
        sb = lambda n, s, t=FP32: ctx.enter_context(nc.sbuf_tensor("r_" + n, s, t))
        pb = lambda n, s, t=FP32: ctx.enter_context(nc.psum_tensor("r_" + n, s, t))
        sem = Sems(nc, ctx)
        settle = sem.settle
        h = sb("h", [128, PER, GS, D])
        xn = sb("xn", [128, PER, GS, D])
        sq = sb("sq", [128, GS, D])
        rows = sb("rows", [128, PER, 4, GS])
        wr1 = sb("wr1", [128, 2 * RH])
        br1 = sb("br1", [2 * RH, 1])
        wr2 = sb("wr2", [2 * RH + 1, 2 * E])
        rh = sb("rh", [2 * RH + 1, 2, N])
        logits = sb("logits", [128, BLOCKS * TOK_BLOCK, E])
        first = sb("first", [128, CS, E])
        pr = sb("pr", [128, 8, CS, E])
        col = sb("col", [128, 8, CS])
        tp = pb("tp", [128, 2, N])
        rp = pb("rp", [2 * RH, 2, N])
        lg = pb("lg", [128, PER, 512])
        (s_set, s_w, s_gset, s_lch, s_cen, s_sq, s_var, s_rt, s_xn, s_tp, s_xt, s_rp, s_rh, s_lg, s_lgc, s_sub,
         s_exp, s_d2, s_e2, s_pch) = (sem(n) for n in [
            "s_set", "s_w", "s_gset", "s_lch", "s_cen", "s_sq", "s_var", "s_rt", "s_xn", "s_tp", "s_xt", "s_rp",
            "s_rh", "s_lg", "s_lgc", "s_sub", "s_exp", "s_d2", "s_e2", "s_pch"])
        s_h = [sem(f"s_h{k}") for k in range(PER)]
        sem.prime()
        W_DMAS = 8
        block = ctx.enter_context(nc.Block())

        def groups(eng):
            with eng.Fori(0, GROUPS // PER) as i:
                for k in range(PER):
                    yield i * PER + k, k, i

        @block.sync
        def _(sp):
            sp.wait_ge(s_set, PRIME + 1)
            row = lambda a: a.rearrange("(a k) -> a k", a=1)
            with nc.allow_non_contiguous_dma(reason="weights, once"):
                for o in range(2):
                    sp.dma_start(wr1[D * o:D * o + D, RH * o:RH * o + RH], d["router_w1"]).then_inc(s_w, 16)
                    sp.dma_start(br1[RH * o:RH * o + RH, :], d["router_b1"].rearrange("(r a) -> r a", a=1)
                                 ).then_inc(s_w, 16)
                    sp.dma_start(wr2[RH * o:RH * o + RH, E * o:E * o + E], d["router_w2"]).then_inc(s_w, 16)
                    sp.dma_start(wr2[2 * RH:2 * RH + 1, E * o:E * o + E], row(d["router_b2"])).then_inc(s_w, 16)
            for g, k, i in groups(sp):
                sp.wait_ge(s_cen, PRIME + g - 1)
                settle(sp)
                sp.dma_start(h[:, k, :, :].rearrange("p (t s) w -> p t (s w)", t=GB), h_v[ds(g * GB, GB)].rearrange(
                    "t p s w -> p t (s w)")).then_inc(s_h[k], 16)

        @block.vector
        def _(dve):
            v = nc.vector
            v.memset(rh[2 * RH:2 * RH + 1, :, :], 1.0)
            v.memset(xt[:, BLOCKS * QUADS:, :], 0.0)
            v.memset(wr1[:, :], 0.0)
            v.memset(wr2[:, :], 0.0).then_inc(s_set, 1)
            bc = lambda a, n, s=GS: a[:, :, None].to_broadcast([128, s, n])
            for g, k, i in groups(dve):
                st = Steps(sem, dve, s_lch, g * 4)
                dve.wait_ge(s_h[k], PRIME + i * 16 + 16)
                hk, xk = h[:, k, :, :], xn[:, k, :, :]
                st(v.tensor_reduce(rows[:, k, 0, :], hk, AX.X, ALU.add))
                st(v.tensor_scalar(rows[:, k, 1, :], rows[:, k, 0, :], 1.0 / D, None, ALU.mult))
                dve.wait_ge(s_tp, PRIME + (g - 1) * GB)
                v.tensor_tensor(xk, hk, bc(rows[:, k, 1, :], D), ALU.subtract).then_inc(s_cen, 1)
                dve.wait_ge(s_sq, PRIME + g + 1)
                st(v.tensor_reduce(rows[:, k, 2, :], sq[:, :, :], AX.X, ALU.add))
                v.tensor_scalar(rows[:, k, 3, :], rows[:, k, 2, :], 1.0 / D, EPS, ALU.mult, ALU.add
                                ).then_inc(s_var, 1)
                dve.wait_ge(s_rt, PRIME + g + 1)
                st(v.reciprocal(rows[:, k, 3, :], rows[:, k, 3, :]))
                v.tensor_tensor(xk, xk, bc(rows[:, k, 3, :], D), ALU.mult).then_inc(s_xn, 1)
                dve.wait_ge(s_lg, PRIME + g * GB + 1)
                settle(dve)
                v.tensor_copy(logits[:, ds(((g + GROUPS - 1) % GROUPS) * GS, GS), :], lg[:, 1 - k, 0:GS * E].rearrange(
                    "p (s e) -> p s e", e=E)).then_inc(s_lgc, 1)
            dve.wait_ge(s_lg, PRIME + GROUPS * GB + 1)
            dve.wait_ge(s_lgc, PRIME + GROUPS)
            v.tensor_copy(logits[:, (GROUPS - 1) * GS:, :], lg[:, 1, 0:GS * E].rearrange("p (s e) -> p s e", e=E)
                          ).then_inc(s_lgc, 1)
            dve.wait_ge(s_lgc, PRIME + GROUPS + 1)
            dve.wait_ge(s_gset, PRIME + 1)
            STEPS = 21
            P_, C_ = (lambda n: pr[:, n, :, :]), (lambda n: col[:, n, :])
            with dve.Fori(0, CHUNKS) as c:
                st = Steps(sem, dve, s_pch, c * STEPS)
                st(v.tensor_copy(P_(0), logits[:, ds(c * CS, CS), :]))
                st(v.tensor_reduce(C_(0), P_(0), AX.X, ALU.max))
                v.tensor_tensor(P_(1), P_(0), bc(C_(0), E, CS), ALU.subtract).then_inc(s_sub, 1)
                dve.wait_ge(s_exp, PRIME + c + 1)
                st(v.tensor_reduce(C_(1), P_(2), AX.X, ALU.add))
                st(v.reciprocal(C_(2), C_(1)))
                st(v.tensor_tensor(P_(3), P_(2), bc(C_(2), E, CS), ALU.mult))
                prob, low = 3, 4
                for n in range(2):
                    st(v.tensor_reduce(C_(3 + n), P_(prob), AX.X, ALU.max))
                    st(v.tensor_tensor(P_(5), P_(prob), bc(C_(3 + n), E, CS), ALU.is_equal))
                    st(v.tensor_tensor(P_(5), P_(5), first[:, :, :], ALU.mult))
                    st(v.tensor_reduce(C_(5), P_(5), AX.X, ALU.max))
                    st(v.tensor_tensor(P_(6 + n), P_(5), bc(C_(5), E, CS), ALU.is_equal))
                    if n == 0:
                        st(v.scalar_tensor_tensor(out=P_(low), in0=P_(6), scalar=-2.0, in1=P_(3),
                                                  op0=ALU.mult, op1=ALU.add))
                        prob = low
                v.tensor_tensor(C_(6), C_(4), C_(3), ALU.subtract).then_inc(s_d2, 1)
                dve.wait_ge(s_e2, PRIME + c + 1)
                st(v.tensor_scalar(C_(0), C_(7), 1.0, None, ALU.add))
                st(v.reciprocal(C_(1), C_(0)))
                st(v.tensor_tensor(C_(2), C_(7), C_(1), ALU.mult))
                v.tensor_tensor(P_(0), P_(6), bc(C_(1), E, CS), ALU.mult)
                st(v.tensor_tensor(P_(1), P_(7), bc(C_(2), E, CS), ALU.mult))
                st(v.tensor_tensor(rw[:, ds(c * CS, CS), :], P_(0), P_(1), ALU.add))
                assert st.n == STEPS, st.n

        @block.gpsimd
        def _(pool):
            nc.gpsimd.iota(first[:, :, :], pattern=[[0, CS], [-1, E]], base=E, channel_multiplier=0,
                           allow_small_or_imprecise_dtypes=True).then_inc(s_gset, 1)

        @block.scalar
        def _(act):
            act.wait_ge(s_w, PRIME + 16 * W_DMAS)
            for g, k, i in groups(act):
                act.wait_ge(s_cen, PRIME + g + 1)
                nc.scalar.activation(sq[:, :, :], xn[:, k, :, :], ACT.Square).then_inc(s_sq, 1)
                act.wait_ge(s_var, PRIME + g + 1)
                nc.scalar.activation(rows[:, k, 3, :], rows[:, k, 3, :], ACT.Sqrt).then_inc(s_rt, 1)

                def turned(b):
                    act.wait_ge(s_tp, PRIME + g * GB + b + 1)
                    settle(act)
                    nc.scalar.copy(xt[:, ds((g * GB + b) * QUADS, QUADS), :], tp[:, b % 2, :].rearrange(
                        "c (i p) -> c i p", p=128)).then_inc(s_xt, 1)

                def hidden(b):
                    act.wait_ge(s_rp, PRIME + g * GB + b + 1)
                    act.wait_ge(s_lg, PRIME + g * GB + b)
                    nc.scalar.activation(rh[0:2 * RH, b % 2, :], rp[:, b % 2, :], ACT.Relu, bias=br1[:, :]
                                         ).then_inc(s_rh, 1)

                turned(0)
                for b in range(1, GB):
                    turned(b)
                    hidden(b - 1)
                hidden(GB - 1)
            with act.Fori(0, CHUNKS) as c:
                act.wait_ge(s_sub, PRIME + c + 1)
                nc.scalar.activation(pr[:, 2, :, :], pr[:, 1, :, :], ACT.Exp).then_inc(s_exp, 1)
                act.wait_ge(s_d2, PRIME + c + 1)
                nc.scalar.activation(col[:, 7, :], col[:, 6, :], ACT.Exp).then_inc(s_e2, 1)

        @block.tensor
        def _(pe):
            mm = nc.tensor.matmul
            pe.wait_ge(s_w, PRIME + 16 * W_DMAS)
            pe.wait_ge(s_set, PRIME + 1)
            for k in range(PER):
                last = mm(lg[:, k, 0:GS * E], ident[:, :], xt[:, BLOCKS * QUADS:, :].rearrange(
                    "c i p -> c (i p)")[:, 0:GS * E], start=True, stop=True)
            last.then_inc(s_lg, 1)
            for g, k, i in groups(pe):
                def turn(b):
                    pe.wait_ge(s_xn, PRIME + g + 1)
                    pe.wait_ge(s_xt, PRIME + g * GB + b - 1)
                    for q in range(QUADS):
                        at0 = TOK_BLOCK * b + 2 * q
                        last = nc.tensor.transpose(tp[:, b % 2, 128 * q:128 * q + 128], xn[:, k, at0:at0 + 2, :]
                                                   .rearrange("p s w -> p (s w)"), ident[:, :])
                    last.then_inc(s_tp, 1)

                def hidden(b):
                    pe.wait_ge(s_rh, PRIME + g * GB + b - 1)
                    pe.wait_ge(s_xt, PRIME + g * GB + b + 1)
                    settle(pe)
                    mm(rp[:, b % 2, :], wr1[:, :], xt[:, ds((g * GB + b) * QUADS, QUADS), :].rearrange(
                        "c i p -> c (i p)"), start=True, stop=True).then_inc(s_rp, 1)

                def score(b):
                    pe.wait_ge(s_rh, PRIME + g * GB + b + 1)
                    pe.wait_ge(s_lgc, PRIME + g)
                    settle(pe)
                    for q in range(QUADS):
                        at0 = (TOK_BLOCK * b + 2 * q) * E
                        last = mm(lg[:, k, at0:at0 + 2 * E], rh[:, b % 2, 128 * q:128 * q + 128], wr2[:, :],
                                  start=True, stop=True)
                    last.then_inc(s_lg, 1)

                turn(0)
                for b in range(1, GB):
                    turn(b)
                    hidden(b - 1)
                    if b > 1:
                        score(b - 2)
                hidden(GB - 1)
                score(GB - 2)
                score(GB - 1)


def experts(nc, d, out, keep):
    EP = E // 2
    PER = 2
    N = 128 * QUADS
    xt, rw = keep["xt_all"], keep["rw"]
    rw_v = rw[:, :, :].rearrange("p (i o) e -> p i o e", o=2)
    blk = lambda a: a.rearrange("(t p s) w -> t p s w", s=TOK_BLOCK, p=128)
    h_v, out_v = blk(d["h1_dram"]), blk(out.rearrange("b n w -> (b n) w"))
    with ExitStack() as ctx:
        sb = lambda n, s, t=FP32: ctx.enter_context(nc.sbuf_tensor("f_" + n, s, t))
        pb = lambda n, s, t=FP32: ctx.enter_context(nc.psum_tensor("f_" + n, s, t))
        sem = Sems(nc, ctx)
        settle = sem.settle
        h = sb("h", [128, PER, QUADS, 2, D])
        res = sb("res", [128, PER, QUADS, 2, D])
        w1 = sb("w1", [128, 2, EP, 128])
        w2 = sb("w2", [128, EP, 128])
        w3 = sb("w3", [128, EP, 128])
        b1 = sb("b1", [128, EP])
        b2 = sb("b2", [128, EP])
        b3 = sb("b3", [128, E, FH])
        a1 = sb("a1", [128, 2, EP, N])
        a2 = sb("a2", [128, 2, EP, N])
        acc = sb("acc", [128, 2, QUADS, D])
        tmp = sb("tmp", [128, QUADS, E, FH])
        mix = sb("mix", [128, QUADS, E, FH])
        got = sb("got", [128, 2, QUADS, D])
        up1 = pb("up1", [128, EP, N])
        up2 = pb("up2", [128, EP, N])
        op = pb("op", [128, 2, 512])
        (s_set, s_w, s_up1, s_up2, s_a1, s_a2, s_op, s_mix, s_sum, s_tmp, s_pch, s_acc, s_res) = (
            sem(n) for n in ["s_set", "s_w", "s_up1", "s_up2", "s_a1", "s_a2", "s_op", "s_mix", "s_sum",
                             "s_tmp", "s_pch", "s_acc", "s_res"])
        s_h, s_st = ([sem(f"{n}{k}") for k in range(PER)] for n in ["s_h", "s_st"])
        sem.prime()
        W_DMAS = 4 * E + 3
        block = ctx.enter_context(nc.Block())

        def tiles(eng):
            with eng.Fori(0, BLOCKS // PER) as i:
                for k in range(PER):
                    for o in range(2):
                        yield (i * PER + k) * 2 + o, i * PER + k, o, k, i

        @block.sync
        def _(sp):
            sp.wait_ge(s_set, PRIME + 1)
            row = lambda a: a.rearrange("(a k) -> a k", a=1)
            with nc.allow_non_contiguous_dma(reason="weights, once"):
                for e in range(E):
                    j, c = e // 2, FH * (e % 2)
                    for o in range(2):
                        sp.dma_start(w1[D * o:D * o + D, o, j, c:c + FH], d["expert_w1"][e]).then_inc(s_w, 16)
                    sp.dma_start(w2[c:c + FH, j, c:c + FH], d["expert_w2"][e]).then_inc(s_w, 16)
                    sp.dma_start(w3[c:c + FH, j, c:c + FH], d["expert_w3"][e]).then_inc(s_w, 16)
                sp.dma_start(b1[:, :], d["expert_b1"].rearrange("(j a) f -> (a f) j", a=2)).then_inc(s_w, 16)
                sp.dma_start(b2[:, :], d["expert_b2"].rearrange("(j a) f -> (a f) j", a=2)).then_inc(s_w, 16)
                sp.dma_start(b3[:, :, :], row(d["expert_b3"].rearrange("e f -> (e f)")).to_broadcast(
                    [128, E * FH])).then_inc(s_w, 16)
            flat = lambda a: a.rearrange("p i o w -> p (i o) w")
            load = lambda t, k: sp.dma_start(flat(h[:, k, :, :, :]), h_v[ds(t, 1)].rearrange(
                "a p s w -> p (a s) w")).then_inc(s_h[k], 16)
            for k in range(PER):
                load(k, k)
            with sp.Fori(0, BLOCKS // PER) as i:
                for k in range(PER):
                    t = i * PER + k
                    sp.wait_ge(s_res, PRIME + (t + 1) * 2)
                    settle(sp)
                    sp.dma_start(out_v[ds(t, 1)].rearrange("a p s w -> p (a s) w"), flat(res[:, k, :, :, :])
                                 ).then_inc(s_st[k], 16)
                    load((t + PER) % BLOCKS, k)
            for k in range(PER):
                sp.wait_ge(s_st[k], PRIME + 16 * (BLOCKS // PER))
                sp.wait_ge(s_h[k], PRIME + 16 * (BLOCKS // PER + 1))

        @block.vector
        def _(dve):
            v = nc.vector
            v.memset(w1[:, :, :, :], 0.0)
            v.memset(w2[:, :, :], 0.0)
            v.memset(w3[:, :, :], 0.0).then_inc(s_set, 1)
            for u, t, o, k, i in tiles(dve):
                def weigh(q):
                    dve.wait_ge(s_sum, PRIME + (u - 1) * QUADS + q + 1)
                    dve.wait_ge(s_op, PRIME + u * QUADS + q + 1)
                    v.tensor_tensor(mix[:, q, :, :], op[:, q % 2, 0:E * FH].rearrange(
                        "p (e f) -> p e f", e=E), rw_v[:, ds(t * QUADS + q, 1), o, :].rearrange(
                        "p a e -> p (a e)")[:, :, None].to_broadcast([128, E, FH]), ALU.mult).then_inc(s_mix, 1)

                def add(q):
                    dve.wait_ge(s_mix, PRIME + u * QUADS + q + 1)
                    v.tensor_reduce(got[:, o, q, :], mix[:, q, :, :].rearrange("p e f -> p f e"), AX.X,
                                    ALU.add).then_inc(s_sum, 1)

                weigh(0)
                dve.wait_ge(s_res, PRIME + u - 1)
                settle(dve)
                for q in range(1, QUADS):
                    weigh(q)
                    add(q - 1)
                add(QUADS - 1)

        @block.gpsimd
        def _(pool):
            g_ = nc.gpsimd
            pool.wait_ge(s_w, PRIME + 16 * W_DMAS)
            for u, t, o, k, i in tiles(pool):
                pool.wait_ge(s_acc, PRIME + u)
                settle(pool)
                for q in range(QUADS):
                    g_.tensor_tensor(tmp[:, q, :, :], b3[:, :, :], rw_v[:, ds(t * QUADS + q, 1), o, :].rearrange(
                        "p a e -> p (a e)")[:, :, None].to_broadcast([128, E, FH]), ALU.mult).then_inc(s_tmp, 1)
                pool.wait_ge(s_tmp, PRIME + (u + 1) * QUADS)
                pool.wait_ge(s_h[k], PRIME + i * 16 + 16)
                settle(pool)
                st = Steps(sem, pool, s_pch, u * (E - 1))
                src = h[:, k, :, o, :]
                for e in range(E):
                    last = g_.tensor_tensor(acc[:, o, :, :], src, tmp[:, :, e, :], ALU.add)
                    src = acc[:, o, :, :]
                    if e < E - 1:
                        st(last)
                last.then_inc(s_acc, 1)
                pool.wait_ge(s_acc, PRIME + u + 1)
                pool.wait_ge(s_sum, PRIME + (u + 1) * QUADS)
                pool.wait_ge(s_st[k], PRIME + i * 16)
                settle(pool)
                g_.tensor_tensor(res[:, k, :, o, :], acc[:, o, :, :], got[:, o, :, :], ALU.add).then_inc(s_res, 1)

        @block.scalar
        def _(act):
            act.wait_ge(s_w, PRIME + 16 * W_DMAS)
            for j in range(EP):
                act.wait_ge(s_up1, PRIME + j + 1)
                nc.scalar.activation(a1[:, 0, j, :], up1[:, j, :], ACT.Relu, bias=b1[:, j:j + 1]).then_inc(s_a1, 1)
            for u, t, o, k, i in tiles(act):
                for j in range(EP):
                    act.wait_ge(s_op, PRIME + (u - 1) * QUADS)
                    act.wait_ge(s_up2, PRIME + u * EP + j + 1)
                    nc.scalar.activation(a2[:, o, j, :], up2[:, j, :], ACT.Relu, bias=b2[:, j:j + 1]
                                         ).then_inc(s_a2, 1)
                    act.wait_ge(s_up1, PRIME + (u + 1) * EP + j + 1)
                    nc.scalar.activation(a1[:, 1 - o, j, :], up1[:, j, :], ACT.Relu, bias=b1[:, j:j + 1]
                                         ).then_inc(s_a1, 1)

        @block.tensor
        def _(pe):
            mm = nc.tensor.matmul
            features = lambda t: xt[:, ds(t * QUADS, QUADS), :].rearrange("c i p -> c (i p)")
            pe.wait_ge(s_w, PRIME + 16 * W_DMAS)
            for j in range(EP):
                mm(up1[:, j, :], w1[:, 0, j, :], xt[:, 0:QUADS, :].rearrange("c i p -> c (i p)"), start=True,
                   stop=True).then_inc(s_up1, 1)
            for u, t, o, k, i in tiles(pe):
                for j in range(EP):
                    pe.wait_ge(s_a2, PRIME + (u - 1) * EP + j + 1)
                    pe.wait_ge(s_a1, PRIME + u * EP + j + 1)
                    mm(up2[:, j, :], w2[:, j, :], a1[:, o, j, :], start=True, stop=True).then_inc(s_up2, 1)
                    mm(up1[:, j, :], w1[:, 1 - o, j, :], features(t + o), start=True, stop=True
                       ).then_inc(s_up1, 1)
                for q in range(QUADS):
                    pe.wait_ge(s_a2, PRIME + u * EP + EP)
                    pe.wait_ge(s_mix, PRIME + u * QUADS + q - 1)
                    for j in range(EP):
                        last = mm(op[:, q % 2, 128 * j:128 * j + 128], a2[:, o, j, 128 * q:128 * q + 128],
                                  w3[:, j, :], start=True, stop=True)
                    last.then_inc(s_op, 1)




def program(nc, d, out):
    nc_dram = lambda n, s, t=FP32: nc.dram_tensor(n, s, t, kind="Internal").ap()
    d["h_dram"] = nc_dram("h_dram", [B, NTOK, D])
    d["tok_dram"] = nc_dram("tok_dram", [B * NTOK, D])
    d["tokc_dram"] = nc_dram("tokc_dram", [B * NTOK, D])
    d["pen_dram"] = nc_dram("pen_dram", [2 * B, TP], BF16)
    d["op_dram"] = nc_dram("op_dram", [2 * B, 128, 6, TP], BF16)
    d["v_dram"] = nc_dram("v_dram", [2 * B, TP, NH * (HD + 1)])
    d["h1_dram"] = nc_dram("h1_dram", [B * NTOK, D])
    with ExitStack() as ctx:
        keep = {}
        sb = lambda n, s, t=FP32: ctx.enter_context(nc.sbuf_tensor(n, s, t))
        keep["nit"] = sb("nit", [1, B], I32)
        keep["ident"] = sb("ident", [128, 128])
        with ExitStack() as early:
            sb = lambda n, s, t=FP32: early.enter_context(nc.sbuf_tensor(n, s, t))
            keep["xn_all"] = sb("xn_all", [128, PAIRS, C + C * W])
            keep["std2"] = sb("std2", [128, PAIRS, C])
            keep["grad"] = sb("grad", [128, PAIRS, C])
            keep["pos"] = sb("pos", [128, PAIRS * C], U32)
            keep["one_rows"] = sb("one_rows", [128, 1])
            conv_norm(nc, d, keep)
            select_keys(nc, d, keep)
            project(nc, d, keep)
        attend(nc, d, keep)
        keep["xt_all"] = ctx.enter_context(nc.sbuf_tensor("xt_all", [128, (BLOCKS + 1) * QUADS, 128], FP32))
        keep["rw"] = ctx.enter_context(nc.sbuf_tensor("rw", [128, BLOCKS * TOK_BLOCK, E], FP32))
        route(nc, d, keep)
        experts(nc, d, out, keep)
_NAMES = ["x", "conv1_w", "conv1_b", "bn_gamma", "bn_beta", "bn_mean", "bn_var", "conv2_w", "conv2_b",
          "w_qkv", "w_proj", "b_proj", "router_w1", "router_b1", "router_w2", "router_b2",
          "expert_w1", "expert_b1", "expert_w2", "expert_b2", "expert_w3", "expert_b3"]


def kernel(**inputs):
    import numpy as _np
    import concourse.bacc as _bacc
    from concourse import mybir as _mybir
    from concourse.bass_utils import run_bass_kernel_spmd as _run

    nc = _bacc.Bacc("TRN2", target_bir_lowering=False, num_devices=1)
    arrays, d = {}, {}
    for full in inputs:
        name = full.replace("L0_tok_", "").replace("L0_attn_", "").replace("L0_ffn_", "")
        a = _np.ascontiguousarray(inputs[full])
        arrays["in_" + name] = a
        d[name] = nc.dram_tensor("in_" + name, a.shape, _mybir.dt.from_np(a.dtype), kind="ExternalInput").ap()
    out = nc.dram_tensor("out", [B, NTOK, D], FP32, kind="ExternalOutput").ap()
    program(nc, d, out)
    return _run(nc, [arrays], core_ids=[0]).results[0]["out"]
```
